# Optimizing a Trainium2 kernel written in Bass

```python
import numpy as np
import jax
import jax.numpy as jnp

def _softmax(x, axis=-1):
    return jax.nn.softmax(x, axis=axis)

def _gelu(x):
    return jax.nn.gelu(x, approximate=True)

def _silu(x):
    return jax.nn.silu(x)

def _sigmoid(x):
    return jax.nn.sigmoid(x)

def _layernorm(x, axis=-1, eps=1e-05):
    m = jnp.mean(x, axis=axis, keepdims=True)
    v = jnp.var(x, axis=axis, keepdims=True)
    return (x - m) / jnp.sqrt(v + eps)

def _scatter_add(tgt, idx, src, axis=0):
    return tgt.at[idx].add(src)

def _segment_sum(src, seg, n):
    return jax.ops.segment_sum(src, seg, n)
kernel_name = 'mk_adj_seq_d1_adj_r2_996739'

def setup_inputs(seed: int=0):
    np.random.seed(seed)
    _w = jnp.asarray

    def _rec_inputs():
        import jax
        import jax.numpy as jnp
        _gk = jax.random.key(seed)
        x = -0.000929 + 1 * jax.random.normal(jax.random.fold_in(_gk, 1), (4096, 128), jnp.float32)
        _a = jax.random.bernoulli(jax.random.fold_in(_gk, 2), 0.000488281, (4096, 4096))
        _a = jnp.logical_or(_a, jnp.swapaxes(_a, -1, -2))
        _a = jnp.logical_or(_a, jnp.eye(4096, dtype=bool))
        adj = _a.astype(jnp.int32)
        return (x, adj)
    x, adj = _rec_inputs()

    def _L0_gnn_setup():
        import jax, jax.numpy as jnp
        import numpy as np
        DIM = 128
        HEADS = 8
        DIM_FF = 512
        N = 2048
        HEAD_DIM = DIM // HEADS
        SCALE = HEAD_DIM ** (-0.5)

        def layer_norm(x, gamma, beta, eps=1e-05):
            mu = jnp.mean(x, axis=-1, keepdims=True)
            var = jnp.var(x, axis=-1, keepdims=True)
            return (x - mu) * jax.lax.rsqrt(var + eps) * gamma + beta
        key = jax.random.key(seed)
        ks = jax.random.split(key, 8)
        x = jax.random.normal(ks[0], (N, DIM), dtype=jnp.float32)
        adj = jax.random.randint(ks[1], (N, N), 0, 2, dtype=jnp.int32)
        adj = adj.at[jnp.arange(N), jnp.arange(N)].set(1)
        s = 1.0 / np.sqrt(DIM)
        w_qkv = jax.random.normal(ks[2], (DIM, 3 * DIM), dtype=jnp.float32) * s
        w_proj = jax.random.normal(ks[3], (DIM, DIM), dtype=jnp.float32) * s
        b_proj = jnp.zeros((DIM,), jnp.float32)
        w1 = jax.random.normal(ks[4], (DIM, DIM_FF), dtype=jnp.float32) * s
        b1 = jnp.zeros((DIM_FF,), jnp.float32)
        w2 = jax.random.normal(ks[5], (DIM_FF, DIM), dtype=jnp.float32) / np.sqrt(DIM_FF)
        b2 = jnp.zeros((DIM,), jnp.float32)
        g1 = jnp.ones((DIM,), jnp.float32)
        be1 = jnp.zeros((DIM,), jnp.float32)
        g2 = jnp.ones((DIM,), jnp.float32)
        be2 = jnp.zeros((DIM,), jnp.float32)
        return {'x': x, 'adj': adj, 'w_qkv': w_qkv, 'w_proj': w_proj, 'b_proj': b_proj, 'w1': w1, 'b1': b1, 'w2': w2, 'b2': b2, 'g1': g1, 'be1': be1, 'g2': g2, 'be2': be2}
    _L0_gnn_all = _L0_gnn_setup()
    _L0_gnn_in = {k: v for k, v in _L0_gnn_all.items() if k in ('w_qkv', 'w_proj', 'b_proj', 'w1', 'b1', 'w2', 'b2', 'g1', 'be1', 'g2', 'be2')}
    del _L0_gnn_all
    return {'x': x, 'adj': adj, 'L0_gnn_w_qkv': _L0_gnn_in['w_qkv'], 'L0_gnn_w_proj': _L0_gnn_in['w_proj'], 'L0_gnn_b_proj': _L0_gnn_in['b_proj'], 'L0_gnn_w1': _L0_gnn_in['w1'], 'L0_gnn_b1': _L0_gnn_in['b1'], 'L0_gnn_w2': _L0_gnn_in['w2'], 'L0_gnn_b2': _L0_gnn_in['b2'], 'L0_gnn_g1': _L0_gnn_in['g1'], 'L0_gnn_be1': _L0_gnn_in['be1'], 'L0_gnn_g2': _L0_gnn_in['g2'], 'L0_gnn_be2': _L0_gnn_in['be2']}

def reference(x, adj, L0_gnn_w_qkv, L0_gnn_w_proj, L0_gnn_b_proj, L0_gnn_w1, L0_gnn_b1, L0_gnn_w2, L0_gnn_b2, L0_gnn_g1, L0_gnn_be1, L0_gnn_g2, L0_gnn_be2):
    import jax
    import jax.numpy as jnp

    def _L0_gnn_ref(x, adj, w_qkv, w_proj, b_proj, w1, b1, w2, b2, g1, be1, g2, be2):
        import jax, jax.numpy as jnp
        import numpy as np
        DIM = 128
        HEADS = 8
        DIM_FF = 512
        N = 2048
        HEAD_DIM = DIM // HEADS
        SCALE = HEAD_DIM ** (-0.5)

        def layer_norm(x, gamma, beta, eps=1e-05):
            mu = jnp.mean(x, axis=-1, keepdims=True)
            var = jnp.var(x, axis=-1, keepdims=True)
            return (x - mu) * jax.lax.rsqrt(var + eps) * gamma + beta
        n = x.shape[0]
        qkv = layer_norm(x, g1, be1) @ w_qkv
        qkv = qkv.reshape(n, 3, HEADS, HEAD_DIM)
        q, k, v = (qkv[:, 0], qkv[:, 1], qkv[:, 2])
        scores = jnp.einsum('nhd,mhd->hnm', q, k) * SCALE
        mask = (adj != 0)[None, :, :]
        scores = jnp.where(mask, scores, -jnp.inf)
        attn = jax.nn.softmax(scores, axis=-1)
        out = jnp.einsum('hnm,mhd->nhd', attn, v).reshape(n, DIM)
        x = x + out @ w_proj + b_proj
        h2 = layer_norm(x, g2, be2)
        ff = jax.nn.gelu(h2 @ w1 + b1) @ w2 + b2
        return x + ff
    x = _L0_gnn_ref(x, adj, L0_gnn_w_qkv, L0_gnn_w_proj, L0_gnn_b_proj, L0_gnn_w1, L0_gnn_b1, L0_gnn_w2, L0_gnn_b2, L0_gnn_g1, L0_gnn_be1, L0_gnn_g2, L0_gnn_be2)
    return x

_drawn_inputs = setup_inputs


def setup_inputs(seed=0):
    import zlib

    import numpy as np

    out = dict(_drawn_inputs(seed))
    spreads = {'L0_gnn_b_proj': (0.0, 0.1),
     'L0_gnn_b1': (0.0, 0.1),
     'L0_gnn_b2': (0.0, 0.1),
     'L0_gnn_g1': (1.0, 0.2),
     'L0_gnn_be1': (0.0, 0.1),
     'L0_gnn_g2': (1.0, 0.2),
     'L0_gnn_be2': (0.0, 0.1)}
    factors = {}
    for name, (base, spread) in spreads.items():
        noise = np.random.default_rng([zlib.crc32(name.encode()), seed]).standard_normal(out[name].shape)
        drawn = base * np.exp(spread * noise) if base else spread * noise
        out[name] = jnp.asarray(drawn.astype(out[name].dtype))
    for name, factor in factors.items():
        out[name] = (out[name] * factor).astype(out[name].dtype)
    return out
```

```python
from contextlib import ExitStack

import concourse.bass as bass
from concourse import mybir


F32 = mybir.dt.float32
BF16 = mybir.dt.bfloat16
I32 = mybir.dt.int32
U32 = mybir.dt.uint32
ALU = mybir.AluOpType
ACT = mybir.ActivationFunctionType
AX_X = mybir.AxisListType.X

P = 128
N = 4096
D = 128
H = 8
DH = D // H
FF = 512
FC = FF // P
NB = N // P
SCALE = float(DH) ** -0.5
EPS = 1e-5
NEG = -1.0e30

SEG = 512
RING = 4
HALF = N // 2
NSEG = HALF // SEG
VSEG = N // SEG
SELF = 1
S1 = SELF + 8
S2 = SELF + 16
COL1 = float(HALF + N - 1)
COL2 = float(2 * N - 1)
NO_ROW = 2 * N


def block_of(tile, b):
    return tile[:, bass.ds(b, 1), :].rearrange("p a d -> p (a d)")


def wait_past(eng, sem, count):
    if not isinstance(count, int) or count > 0:
        eng.wait_ge(sem, count)


def over_heads(tile, slots):
    return tile.rearrange("p (s a) -> p s a", a=1).to_broadcast([P, slots, H])


def over_slots(tile, slots):
    return tile.rearrange("p (a h) -> p a h", a=1).to_broadcast([P, slots, H])


def graph_layer(nc, x, adj, w_qkv, w_proj, b_proj, w1, b1, w2, b2, g1, be1, g2, be2, out, force_dense=False):
    kv_dram = nc.dram_tensor("kv_table", [N, 2 * D], F32).ap()
    q_dram = nc.dram_tensor("q_table", [N, D], F32).ap()
    x_rows = x.rearrange("(b p) d -> p b d", p=P)
    out_rows = out.rearrange("(b p) d -> b p d", p=P)
    adj_rows = adj.rearrange("(b p) m -> b p m", p=P)
    kv_rows = kv_dram.rearrange("(b p) d -> b p d", p=P)

    ctx = ExitStack()
    with ctx:
        def sb(name, shape, dt=F32):
            return ctx.enter_context(nc.sbuf_tensor(name, shape, dt))

        def sem(name):
            return ctx.enter_context(nc.semaphore(name))

        ident = sb("ident", [P, P])
        ident_1 = sb("ident_1", [P, P], BF16)
        ident_2 = sb("ident_2", [P, P], BF16)
        ones33 = sb("ones33", [33, P], BF16)
        column_key = sb("column_key", [33, N], BF16)
        ones = sb("ones", [P, P])
        before = sb("before", [P, P])
        rank = sb("rank", [P, P])
        row_number = sb("row_number", [P, NB])
        self_key = sb("self_key", [P, NB])
        head_cols = sb("head_cols", [P, H])
        consts = sb("consts", [P, 5])
        eps_col, col1, half_col, col2, n_col = (consts[:, i:i + 1] for i in range(5))
        wqkv_sb = sb("wqkv_sb", [P, 3 * D])
        wproj_sb = sb("wproj_sb", [P, D])
        w1_sb = sb("w1_sb", [P, FF])
        w2_sb = sb("w2_sb", [P, FC, D])
        bproj_row = sb("bproj_row", [1, D])
        b2_row = sb("b2_row", [1, D])
        b1_col = sb("b1_col", [P, FC])
        ln_cols = sb("ln_cols", [P, 4])
        diag = sb("diag", [P, NB], I32)

        xs = sb("xs", [P, NB + 1, D])
        qs = sb("qs", [P, NB, D])
        slots = sb("slots", [P, 2 * S1 + S2, 2 * D])
        vq = sb("vq", [P, 1, D])
        adj_sb = sb("adj_sb", [P, 2, N], I32)
        mask = sb("mask", [P, 2, N], BF16)

        stats = sb("stats", [P, NB + 1, 6])
        mean = sb("mean", [P, NB + 1])
        var = sb("var", [P, NB + 1])
        half = sb("half", [P, NB + 1])
        rstd = sb("rstd", [P, NB + 1])
        shift = sb("shift", [P, NB + 1])
        xn = sb("xn", [P, 2, D])
        xnT = sb("xnT", [P, 2, 4 * P])

        cand = sb("cand", [P, NSEG * 8])
        clean = sb("clean", [P, 2, NSEG * 8])
        found = sb("found", [P, NB, NSEG * 8])
        top = sb("top", [P, 2, 8])
        gap = sb("gap", [P, 2, S1])
        idx = sb("idx", [P, 2, 8], I32)
        self_gap = sb("self_gap", [P, NB])
        vcand = sb("vcand", [P, VSEG * 8])
        vclean = sb("vclean", [P, VSEG * 8])
        vrest = sb("vrest", [P, VSEG * 8])
        vtop = sb("vtop", [P, 16])
        vgap = sb("vgap", [P, S2])
        vidx = sb("vidx", [P, 16], I32)
        flag = sb("flag", [P, NB])
        work = sb("work", [P, NB, NSEG * 8])
        count = sb("count", [P, NB])
        full = sb("full", [P, NB, NSEG])
        worst = sb("worst", [P, NB])
        totals = sb("totals", [P, NB])
        place = sb("place", [P, NB])
        pick = sb("pick", [P, 2, P])
        vnum = sb("vnum", [P, 4])
        vrow = sb("vrow", [P, 1], I32)
        vwork = sb("vwork", [P, VSEG * 8])
        vstat = sb("vstat", [P, 6])
        dense_flag = sb("dense_flag", [P, 1], I32)

        prod = sb("prod", [P, S2, D])
        sc = sb("sc", [P, S2, H])
        smax = sb("smax", [P, H])
        ex = sb("ex", [P, S2, H])
        den = sb("den", [P, H])
        rden = sb("rden", [P, H])
        pr = sb("pr", [P, S2, H])
        pv0 = sb("pv0", [P, S2, D])
        pv1 = sb("pv1", [P, S1, D])
        pv = (pv0, pv1)
        oT = sb("oT", [P, 2, P])
        gT = sb("gT", [P, FC, 4 * P])
        res = sb("res", [P, 2, 4, D])
        ps = ctx.enter_context(nc.psum_tensor("ps", [P, 8, 512], F32))

        s_const = sem("s_const")
        s_weights = sem("s_weights")
        s_diag = sem("s_diag")
        s_x = sem("s_x")
        s_adj = [sem("s_adj0"), sem("s_adj1")]
        s_stats = sem("s_stats")
        s_aggr = sem("s_aggr")
        s_sqrt = sem("s_sqrt")
        s_rstd = sem("s_rstd")
        s_shift = sem("s_shift")
        s_xn = sem("s_xn")
        s_xnT_ps = sem("s_xnT_ps")
        s_xnT = sem("s_xnT")
        s_qkv_ps = sem("s_qkv_ps")
        s_q = sem("s_q")
        s_kv = sem("s_kv")
        s_kv_stored = sem("s_kv_stored")
        s_q_stored = sem("s_q_stored")
        s_self = [sem("s_self0"), sem("s_self1")]
        s_mask = sem("s_mask")
        s_keys = sem("s_keys")
        s_cand = sem("s_cand")
        s_clean = sem("s_clean")
        s_top = sem("s_top")
        s_idx = sem("s_idx")
        s_gap = sem("s_gap")
        s_gather = [sem("s_gather0"), sem("s_gather1")]
        s_flag = sem("s_flag")
        s_flag_ps = sem("s_flag_ps")
        s_pick = sem("s_pick")
        s_pick_ps = sem("s_pick_ps")
        s_vnum = sem("s_vnum")
        s_vrow = sem("s_vrow")
        s_vadj = sem("s_vadj")
        s_vload = sem("s_vload")
        s_vsearch = sem("s_vsearch")
        s_vcheck = sem("s_vcheck")
        s_vcheck_ps = sem("s_vcheck_ps")
        s_dense = sem("s_dense")
        s_score = sem("s_score")
        s_exp = sem("s_exp")
        s_soft = sem("s_soft")
        s_pv = sem("s_pv")
        s_oT_ps = sem("s_oT_ps")
        s_oT = sem("s_oT")
        s_x2_ps = sem("s_x2_ps")
        s_x2 = sem("s_x2")
        s_u_ps = sem("s_u_ps")
        s_g = sem("s_g")
        s_ff = sem("s_ff")
        s_res = sem("s_res")
        s_out = [sem("s_out0"), sem("s_out1")]
        s_vout = sem("s_vout")

        d_load = sem("d_load")
        d_copied = sem("d_copied")
        d_kT_ps = sem("d_kT_ps")
        d_kT = sem("d_kT")
        d_x = sem("d_x")
        d_adj_free = sem("d_adj_free")
        d_adj = sem("d_adj")
        d_bias = sem("d_bias")
        d_q = sem("d_q")
        d_qT_ps = sem("d_qT_ps")
        d_qT = sem("d_qT")
        d_qh = sem("d_qh")
        d_s_ps = sem("d_s_ps")
        d_s = sem("d_s")
        d_max = sem("d_max")
        d_neg = sem("d_neg")
        d_exp = sem("d_exp")
        d_rden = sem("d_rden")
        d_pT_ps = sem("d_pT_ps")
        d_pT = sem("d_pT")
        d_o_ps = sem("d_o_ps")
        d_o = sem("d_o")
        d_oT_ps = sem("d_oT_ps")
        d_oT = sem("d_oT")
        d_x2_ps = sem("d_x2_ps")
        d_x2 = sem("d_x2")
        d_norow = sem("d_norow")

        kT = slots[:, 0:16, :].rearrange("p s d -> p (s d)")
        v_all = slots[:, 16:32, :].rearrange("p s (a d) -> p (s a) d", a=2)
        bias = adj_sb[:, 1, :].bitcast(F32)
        s_all = mask[:, :, :].rearrange("p a m -> p (a m)").bitcast(F32)
        pT = gT[:, 0:2, :]
        att = prod[:, 0, :]
        TURNS = 8

        block = ctx.enter_context(nc.Block())

        def where_dense(eng):
            eng.wait_ge(s_dense, 1)
            eng.wait_ge(s_x2, NB + 1)
            return eng.If(eng.value_load(dense_flag[0:1, 0:1], min_val=0, max_val=1) > 0)
        NWEIGHTS = 11
        NCONST = 25
        HALF_STORE = NB // 4
        SCORE_STEPS = 5
        FLAG_STEPS = 14
        ALL_KEYS = NSEG * NB

        def slot_tile(b, j):
            if isinstance(b, int) and b == NB:
                return slots[:, 2 * S1:2 * S1 + S2, :], S2
            return slots[:, S1 * j:S1 * (j + 1), :], S1

        @block.sync
        def _(sp):
            sp.dma_start(xs[:, 0:NB, :], x_rows).then_inc(s_x, 16)
            sp.dma_start(adj_sb[:, 0, :], adj_rows[0, :, :]).then_inc(s_adj[0], 16)
            sp.dma_start(adj_sb[:, 1, :], adj_rows[1, :, :]).then_inc(s_adj[1], 16)
            for c in range(4):
                sp.wait_ge(s_kv, HALF_STORE * (c + 1))
                sp.dma_start(kv_rows[HALF_STORE * c:HALF_STORE * (c + 1), :, :].rearrange("b p d -> p b d"),
                             slots[:, HALF_STORE * c:HALF_STORE * (c + 1), :]).then_inc(s_kv_stored, 16)
            sp.wait_ge(s_q, NB)
            sp.dma_start(q_dram.rearrange("(b p) d -> p b d", p=P), qs[:, :, :]).then_inc(s_q_stored, 16)
            sp.wait_ge(s_kv_stored, 64)

            def load_adj(b, j):
                sp.wait_ge(s_mask, b - 1)
                sp.dma_start(adj_sb[:, j, :], adj_rows[b, :, :]).then_inc(s_adj[j], 16)

            def load_self(b, j):
                wait_past(sp, s_pv, b - 1)
                sp.dma_start(slots[:, S1 * j, :], kv_rows[b, :, :]).then_inc(s_self[j], 16)

            load_self(0, 0)
            load_self(1, 1)
            load_adj(2, 0)
            load_adj(3, 1)
            load_adj(4, 0)
            load_self(2, 0)
            load_adj(5, 1)
            load_self(3, 1)
            with sp.Fori(3, NB // 2) as i:
                for j in range(2):
                    load_adj(2 * i + j, j)
                    load_self(2 * i + j - 2, j)
            load_self(NB - 2, 0)
            load_self(NB - 1, 1)

            with where_dense(sp):
                kv_cols = kv_dram.rearrange("(b p) d -> p b d", p=P)
                sp.dma_start(xs[:, 0:NB, :], kv_cols[:, :, 0:D]).then_inc(d_load, 16)
                sp.dma_start(v_all, kv_cols[:, :, D:2 * D]).then_inc(d_load, 16)
                sp.wait_ge(d_copied, NB)
                sp.dma_start(xs[:, 0:NB, :], x_rows).then_inc(d_x, 16)
                with sp.Fori(0, NB) as b:
                    sp.wait_ge(d_adj_free, b + 1)
                    sp.dma_start(adj_sb[:, 0, :], adj_rows[b, :, :]).then_inc(d_adj, 16)
                sp.wait_ge(d_x2, NB)

            with sp.Fori(0, NB // 8) as i:
                for j in range(2):
                    g = 2 * i + j
                    sp.wait_ge(s_res, 4 * g + 4)
                    sp.dma_start(out_rows[bass.ts(g, 4), :, :].rearrange("b p d -> p b d"),
                                 res[:, j, :, :]).then_inc(s_out[j], 16)
            for j in range(2):
                sp.wait_ge(s_out[j], 16 * (NB // 8))

        @block.gpsimd
        def _(pool):
            made = [0]

            def step(instruction):
                made[0] += 1
                instruction.then_inc(s_const, 1)
                pool.wait_ge(s_const, made[0])

            step(pool.memset(ident[:, :], 0.0))
            step(pool.affine_select(out=ident[:, :], in_=ident[:, :], compare_op=ALU.not_equal, fill=1.0,
                                    base=0, pattern=[[-1, P]], channel_multiplier=1))
            for tile, value in ((ident_1, float(HALF)), (ident_2, float(N))):
                step(pool.memset(tile[:, :], 0.0))
                step(pool.affine_select(out=tile[:, :], in_=tile[:, :], compare_op=ALU.not_equal, fill=value,
                                        base=0, pattern=[[-1, P]], channel_multiplier=1))
            step(pool.memset(ones33[:, :], 1.0))
            step(pool.memset(ones[:, :], 1.0))
            for col, value in ((eps_col, EPS), (col1, COL1), (half_col, float(HALF)), (col2, COL2), (n_col, float(N))):
                step(pool.memset(col, value))
            step(pool.memset(column_key[:, :], 0.0))
            step(pool.iota(column_key[0:1, :], pattern=[[-64, N // 64], [0, 64]], base=N - 64, channel_multiplier=0,
                           allow_small_or_imprecise_dtypes=True))
            step(pool.iota(column_key[32:33, :], pattern=[[0, N // 64], [-1, 64]], base=63, channel_multiplier=0,
                           allow_small_or_imprecise_dtypes=True))
            step(pool.memset(slots[:, NB:2 * S1 + S2, :], 0.0))
            step(pool.affine_select(out=before[:, :], in_=ones[:, :], compare_op=ALU.is_gt, fill=0.0,
                                    base=0, pattern=[[1, P]], channel_multiplier=-1))
            step(pool.iota(rank[:, :], pattern=[[1, P]], base=1, channel_multiplier=0,
                           allow_small_or_imprecise_dtypes=True))
            step(pool.iota(row_number[:, :], pattern=[[P, NB]], base=1, channel_multiplier=1,
                           allow_small_or_imprecise_dtypes=True))
            step(pool.affine_select(out=head_cols[:, :], in_=ones[:, 0:H], compare_op=ALU.is_ge, fill=0.0,
                                    base=0, pattern=[[-DH, H]], channel_multiplier=1))
            step(pool.affine_select(out=head_cols[:, :], in_=head_cols[:, :], compare_op=ALU.is_ge, fill=0.0,
                                    base=DH - 1, pattern=[[DH, H]], channel_multiplier=-1))
            step(pool.iota(self_key[:, :], pattern=[[-P, NB]], base=int(COL1), channel_multiplier=-1,
                           allow_small_or_imprecise_dtypes=True))
            step(pool.memset(xs[:, NB, :], 0.0))
            step(pool.memset(vq[:, 0, :], 0.0))
            assert made[0] == NCONST, made[0]

            def gather_rows(dst, table, row, sem):
                pool.indirect_dma_start(out=dst, out_offset=None, in_=table,
                                        in_offset=bass.IndirectOffsetOnAxis(ap=row.bitcast(U32), axis=0),
                                        bounds_check=N - 1, oob_is_err=False).then_inc(sem, 16)

            def gather(b, j):
                pool.wait_ge(s_idx, b + 1)
                wait_past(pool, s_pv, b - 1)
                pool.nop(nofuse=True)
                for s in range(8):
                    gather_rows(slots[:, S1 * j + SELF + s, :], kv_dram[:, :], idx[:, j, s:s + 1], s_gather[j])

            pool.wait_ge(s_kv_stored, 64)
            gather(0, 0)
            gather(1, 1)
            with pool.Fori(1, NB // 2) as i:
                for j in range(2):
                    gather(2 * i + j, j)

            pool.wait_ge(s_vrow, 1)
            pool.wait_ge(s_mask, NB - 1)
            pool.wait_ge(s_q_stored, 16)
            gather_rows(adj_sb[:, 0, :], adj[:, :], vrow[:, 0:1], s_vadj)
            gather_rows(slots[:, 2 * S1, :], kv_dram[:, :], vrow[:, 0:1], s_vload)
            gather_rows(vq[:, 0, :], q_dram[:, :], vrow[:, 0:1], s_vload)
            gather_rows(xs[:, NB, :], x[:, :], vrow[:, 0:1], s_vload)
            pool.wait_ge(s_idx, NB + 1)
            for s in range(16):
                gather_rows(slots[:, 2 * S1 + SELF + s, :], kv_dram[:, :], vidx[:, s:s + 1], s_gather[0])

            with where_dense(pool):
                pool.memset(vrow[:, :], NO_ROW).then_inc(d_norow, 1)
                pool.wait_ge(d_norow, 1)
                pool.wait_ge(d_x2, NB)

            for j in range(2):
                pool.wait_ge(s_out[j], 16 * (NB // 8))
            pool.wait_ge(s_res, NB + 1)
            pool.indirect_dma_start(out=out[:, :], out_offset=bass.IndirectOffsetOnAxis(
                ap=vrow[:, 0:1].bitcast(U32), axis=0), in_=res[:, 0, 0, :], in_offset=None,
                bounds_check=N - 1, oob_is_err=False).then_inc(s_vout, 16)
            pool.wait_ge(s_vout, 16)

        @block.scalar
        def _(act):
            for dst, src in ((wqkv_sb[:, :], w_qkv), (wproj_sb[:, :], w_proj), (w1_sb[:, :], w1),
                             (w2_sb[:, :, :], w2.rearrange("(c p) n -> p c n", p=P)),
                             (bproj_row[:, :], b_proj.rearrange("(a n) -> a n", a=1)),
                             (b2_row[:, :], b2.rearrange("(a n) -> a n", a=1)),
                             (b1_col[:, :], b1.rearrange("(c p) -> p c", p=P)),
                             (ln_cols[:, 0:1], g1.rearrange("(p a) -> p a", a=1)),
                             (ln_cols[:, 1:2], be1.rearrange("(p a) -> p a", a=1)),
                             (ln_cols[:, 2:3], g2.rearrange("(p a) -> p a", a=1)),
                             (ln_cols[:, 3:4], be2.rearrange("(p a) -> p a", a=1))):
                act.dma_start(dst, src, allow_slow_non_contiguous=True).then_inc(s_weights, 16)
            act.dma_start(diag[:, :], bass.AP(tensor=adj.tensor, offset=0, ap=[[N + 1, P], [P * (N + 1), NB]]),
                          allow_slow_non_contiguous=True).then_inc(s_diag, 16)
            act.wait_ge(s_const, NCONST)

            def standard_deviation(rnd, width):
                act.wait_ge(s_aggr, 6 * (rnd + 1))
                act.activation(rstd[:, 0:width], var[:, 0:width], ACT.Sqrt, bias=eps_col).then_inc(s_sqrt, 1)
                act.wait_ge(s_shift, rnd + 1)

            def normalise(b, j):
                act.activation(xn[:, j, :], block_of(xs, b), ACT.Identity, bias=shift[:, bass.ds(b, 1)],
                               scale=rstd[:, bass.ds(b, 1)]).then_inc(s_xn, 1)

            standard_deviation(0, NB)

            def keep_q(b, j):
                act.wait_ge(s_qkv_ps, b + 1)
                act.activation(block_of(qs, b), ps[:, 2 + j, 0:D], ACT.Copy).then_inc(s_q, 1)

            normalise(0, 0)
            normalise(1, 1)
            with act.Fori(1, NB // 2) as i:
                for j in range(2):
                    b = 2 * i + j
                    act.wait_ge(s_xnT_ps, b - 1)
                    normalise(b, j)
                    keep_q(b - 2, j)
            keep_q(NB - 2, 0)
            keep_q(NB - 1, 1)

            def make_mask(b, j):
                act.wait_ge(s_adj[j], 8 * (b - j) + 16)
                wait_past(act, s_keys, NSEG * (b - 1))
                act.activation(mask[:, j, :], adj_sb[:, j, :], ACT.Square).then_inc(s_mask, 1)

            def slot_numbers(b, j):
                act.wait_ge(s_top, b + 1)
                wait_past(act, s_gather[j], 8 * 8 * (b - j))
                act.activation(idx[:, j, :], top[:, j, :], ACT.Relu, scale=-1.0, bias=col1).then_inc(s_idx, 1)
                wait_past(act, s_score, SCORE_STEPS * (b - 1))
                act.activation(gap[:, j, SELF:S1], top[:, j, :], ACT.Relu, scale=-1.0, bias=half_col).then_inc(s_gap, 1)
                act.activation(gap[:, j, 0:1], self_gap[:, bass.ds(b, 1)], ACT.Copy).then_inc(s_gap, 1)
                act.activation(block_of(found, b), clean[:, j, :], ACT.Copy).then_inc(s_gap, 1)

            def exponentials(b, slots_n=S1):
                act.wait_ge(s_score, SCORE_STEPS * (b + 1))
                wait_past(act, s_soft, 3 * b)
                act.activation(ex[:, 0:slots_n, :], sc[:, 0:slots_n, :], ACT.Exp, scale=SCALE).then_inc(s_exp, 1)

            def attention_out(b, j):
                act.wait_ge(s_oT_ps, b + 1)
                act.activation(oT[:, j, :], ps[:, 0, 0:P], ACT.Copy).then_inc(s_oT, 1)
                act.wait_ge(s_x2_ps, b + 1)
                act.activation(block_of(xs, b), ps[:, 2, 0:D], ACT.Copy).then_inc(s_x2, 1)

            make_mask(0, 0)
            make_mask(1, 1)
            act.wait_ge(s_flag, 1)
            slot_numbers(0, 0)
            make_mask(2, 0)
            slot_numbers(1, 1)
            make_mask(3, 1)
            exponentials(0)
            slot_numbers(2, 0)
            make_mask(4, 0)
            exponentials(1)
            slot_numbers(3, 1)
            attention_out(0, 0)
            with act.Fori(2, NB // 2 - 1) as i:
                for j in range(2):
                    b = 2 * i + j
                    make_mask(b + 1, 1 - j)
                    exponentials(b - 2)
                    slot_numbers(b, j)
                    attention_out(b - 3, 1 - j)
            make_mask(NB - 1, 1)
            exponentials(NB - 4)
            slot_numbers(NB - 2, 0)
            attention_out(NB - 5, 1)
            exponentials(NB - 3)
            slot_numbers(NB - 1, 1)
            attention_out(NB - 4, 0)
            exponentials(NB - 2)
            attention_out(NB - 3, 1)
            exponentials(NB - 1)
            attention_out(NB - 2, 0)
            attention_out(NB - 1, 1)

            act.wait_ge(s_vadj, 16)
            act.activation(mask[:, 0, :], adj_sb[:, 0, :], ACT.Square).then_inc(s_mask, 1)
            act.wait_ge(s_top, NB + 1)
            act.activation(vidx[:, :], vtop[:, :], ACT.Relu, scale=-1.0, bias=col2).then_inc(s_idx, 1)
            act.activation(vgap[:, SELF:S2], vtop[:, :], ACT.Relu, scale=-1.0, bias=n_col).then_inc(s_gap, 1)
            exponentials(NB, S2)
            attention_out(NB, 0)

            with where_dense(act):
                act.wait_ge(d_load, 32)
                with act.Fori(0, NB) as c:
                    act.activation(xn[:, 0, :], block_of(xs, c), ACT.Copy).then_inc(d_copied, 1)
                    act.wait_ge(d_kT_ps, c + 1)
                    act.activation(kT[:, bass.ts(c, P)], ps[:, 0, 0:P], ACT.Copy).then_inc(d_kT, 1)
                with act.Fori(0, NB) as b:
                    act.activation(xn[:, 1, :], block_of(qs, b), ACT.Copy).then_inc(d_q, 1)
                    act.wait_ge(d_qT_ps, b + 1)
                    act.activation(xnT[:, 0, 0:P], ps[:, 1, 0:P], ACT.Copy).then_inc(d_qT, 1)
                    with act.Fori(0, H) as h:
                        act.wait_ge(d_neg, H * b + h + 1)
                        act.activation(s_all, s_all, ACT.Exp, scale=SCALE, bias=smax[:, 1:2],
                                       accum_out=den[:, 0:1]).then_inc(d_exp, 1)
                    act.wait_ge(d_oT_ps, b + 1)
                    act.activation(oT[:, 0, :], ps[:, 0, 0:P], ACT.Copy).then_inc(d_oT, 1)
                    act.wait_ge(d_x2_ps, b + 1)
                    act.activation(block_of(xs, b), ps[:, 2, 0:D], ACT.Copy).then_inc(d_x2, 1)

            standard_deviation(1, NB + 1)

            def gelu_up(g, width):
                for c in range(FC):
                    act.wait_ge(s_u_ps, FC * g + c + 1)
                    act.activation(gT[:, c, 0:width * P], ps[:, 4 + c, 0:width * P], ACT.Gelu_apprx_tanh,
                                   bias=b1_col[:, c:c + 1]).then_inc(s_g, 1)

            with act.Fori(0, NB // 4) as g:
                for r in range(4):
                    act.wait_ge(s_xnT_ps, NB + 4 * g + r - 1)
                    normalise(4 * g + r, r % 2)
                gelu_up(g, 4)
            act.wait_ge(s_xnT_ps, 2 * NB - 1)
            normalise(NB, 0)
            gelu_up(NB // 4, 1)

        @block.vector
        def _(dve):
            def statistics(rnd, width):
                with dve.Fori(0, width) as b:
                    if rnd:
                        dve.wait_ge(s_x2, b + 1)
                    dve.bn_stats(block_of(stats, b), block_of(xs, b)).then_inc(s_stats, 1)
                dve.wait_ge(s_stats, width + NB * rnd)
                even, odd = stats[:, 0:width, 1], stats[:, 0:width, 4]
                w = slice(0, width)
                dve.tensor_tensor(mean[:, w], even, odd, ALU.add).then_inc(s_aggr, 1)
                dve.tensor_tensor(half[:, w], even, odd, ALU.subtract).then_inc(s_aggr, 1)
                dve.tensor_tensor(var[:, w], stats[:, w, 2], stats[:, w, 5], ALU.add).then_inc(s_aggr, 1)
                dve.wait_ge(s_aggr, 6 * rnd + 3)
                dve.tensor_scalar(mean[:, w], mean[:, w], -0.5, None, ALU.mult).then_inc(s_aggr, 1)
                dve.scalar_tensor_tensor(out=half[:, w], in0=half[:, w], scalar=0.25, in1=half[:, w],
                                         op0=ALU.mult, op1=ALU.mult).then_inc(s_aggr, 1)
                dve.wait_ge(s_aggr, 6 * rnd + 5)
                dve.scalar_tensor_tensor(out=var[:, w], in0=var[:, w], scalar=1.0 / D, in1=half[:, w],
                                         op0=ALU.mult, op1=ALU.add).then_inc(s_aggr, 1)
                dve.wait_ge(s_sqrt, rnd + 1)
                dve.reciprocal(rstd[:, w], rstd[:, w]).then_inc(s_rstd, 1)
                dve.wait_ge(s_rstd, rnd + 1)
                dve.tensor_tensor(shift[:, w], mean[:, w], rstd[:, w], ALU.mult).then_inc(s_shift, 1)

            dve.wait_ge(s_x, 16)
            statistics(0, NB)
            dve.wait_ge(s_weights, 16 * NWEIGHTS)
            dve.wait_ge(s_diag, 16)
            dve.tensor_scalar(self_gap[:, :], diag[:, :], 0.0, None, ALU.is_equal).then_inc(s_flag, 1)

            def keep_xnT(b, j):
                dve.wait_ge(s_xnT_ps, b + 1)
                wait_past(dve, s_qkv_ps, b - 1)
                dve.tensor_scalar(xnT[:, j, 0:P], ps[:, j, 0:P], ln_cols[:, 0:1], ln_cols[:, 1:2],
                                  ALU.mult, ALU.add).then_inc(s_xnT, 1)

            def keep_kv(b, j):
                dve.wait_ge(s_qkv_ps, b + 1)
                dve.tensor_copy(block_of(slots, b), ps[:, 6 + j, 0:2 * D]).then_inc(s_kv, 1)

            keep_xnT(0, 0)
            keep_xnT(1, 1)
            with dve.Fori(1, NB // 2) as i:
                for j in range(2):
                    keep_kv(2 * i + j - 2, j)
                    keep_xnT(2 * i + j, j)
            keep_kv(NB - 2, 0)
            keep_kv(NB - 1, 1)

            def extract(b, j):
                for s in range(NSEG):
                    dve.wait_ge(s_keys, NSEG * b + s + 1)
                    dve.nop(nofuse=True)
                    dve.max(out=cand[:, 8 * s:8 * s + 8], in_=ps[:, 4 + s % RING, :]).then_inc(s_cand, 1)
                dve.wait_ge(s_cand, NSEG * (b + 1))
                wait_past(dve, s_gap, 3 * (b - 1))
                dve.scalar_tensor_tensor(out=clean[:, j, :], in0=cand[:, :], scalar=self_key[:, bass.ds(b, 1)],
                                         in1=cand[:, :], op0=ALU.not_equal, op1=ALU.mult).then_inc(s_clean, 1)
                dve.wait_ge(s_clean, b + 1)
                dve.nop(nofuse=True)
                dve.max(out=top[:, j, :], in_=clean[:, j, :]).then_inc(s_top, 1)

            def scores(b, j, q, gaps):
                tile, n = slot_tile(b, j)
                dve.tensor_tensor(prod[:, 0:n, :], tile[:, :, 0:D], q.to_broadcast([P, n, D]),
                                  ALU.mult).then_inc(s_score, 1)
                dve.wait_ge(s_score, SCORE_STEPS * b + 1)
                wait_past(dve, s_exp, b)
                dve.tensor_reduce(sc[:, 0:n, :].rearrange("p s h -> p (s h)"),
                                  prod[:, 0:n, :].rearrange("p s (h e) -> p (s h) e", e=DH),
                                  axis=AX_X, op=ALU.add).then_inc(s_score, 1)
                dve.wait_ge(s_score, SCORE_STEPS * b + 2)
                dve.scalar_tensor_tensor(out=sc[:, 0:n, :], in0=over_heads(gaps, n), scalar=NEG, in1=sc[:, 0:n, :],
                                         op0=ALU.mult, op1=ALU.add).then_inc(s_score, 1)
                dve.wait_ge(s_score, SCORE_STEPS * b + 3)
                dve.tensor_reduce(smax[:, :], sc[:, 0:n, :].rearrange("p s h -> p h s"), axis=AX_X,
                                  op=ALU.max).then_inc(s_score, 1)
                dve.wait_ge(s_score, SCORE_STEPS * b + 4)
                dve.tensor_tensor(sc[:, 0:n, :], sc[:, 0:n, :], over_slots(smax[:, :], n),
                                  ALU.subtract).then_inc(s_score, 1)

            def block_scores(b, j):
                dve.wait_ge(s_gather[j], 64 * (b - j) + 128)
                dve.wait_ge(s_self[j], 8 * (b - j) + 16)
                dve.wait_ge(s_gap, 3 * (b + 1))
                scores(b, j, qs[:, bass.ds(b, 1), :], gap[:, j, :])

            def weigh_values(b, j):
                tile, n = slot_tile(b, j)
                dve.wait_ge(s_exp, b + 1)
                dve.tensor_reduce(den[:, :], ex[:, 0:n, :].rearrange("p s h -> p h s"), axis=AX_X,
                                  op=ALU.add).then_inc(s_soft, 1)
                dve.wait_ge(s_soft, 3 * b + 1)
                dve.reciprocal(rden[:, :], den[:, :]).then_inc(s_soft, 1)
                dve.wait_ge(s_soft, 3 * b + 2)
                dve.tensor_tensor(pr[:, 0:n, :], ex[:, 0:n, :], over_slots(rden[:, :], n),
                                  ALU.mult).then_inc(s_soft, 1)
                dve.wait_ge(s_soft, 3 * b + 3)
                wait_past(dve, s_oT_ps, b - 1)
                dve.tensor_tensor(pv[j][:, 0:n, :].rearrange("p s (h e) -> p s h e", e=DH),
                                  tile[:, :, D:2 * D].rearrange("p s (h e) -> p s h e", e=DH),
                                  pr[:, 0:n, :].rearrange("p s (h a) -> p s h a", a=1).to_broadcast([P, n, H, DH]),
                                  ALU.mult).then_inc(s_pv, 1)

            extract(0, 0)
            extract(1, 1)
            dve.wait_ge(s_q, NB)
            for b in (2, 3):
                block_scores(b - 2, b % 2)
                extract(b, b % 2)
                weigh_values(b - 2, b % 2)
            with dve.Fori(2, NB // 2) as i:
                for j in range(2):
                    b = 2 * i + j
                    block_scores(b - 2, j)
                    extract(b, j)
                    weigh_values(b - 2, j)

            flagged = [1]

            def link(instruction):
                flagged[0] += 1
                instruction.then_inc(s_flag, 1)
                dve.wait_ge(s_flag, flagged[0])

            dve.wait_ge(s_gap, 3 * NB)
            link(dve.tensor_scalar(work[:, :, :], found[:, :, :], float(HALF), None, ALU.is_ge))
            link(dve.tensor_reduce(full[:, :, :], work[:, :, :].rearrange("p b (s k) -> p b s k", k=8), axis=AX_X,
                                   op=ALU.add))
            link(dve.tensor_reduce(count[:, :], full[:, :, :], axis=AX_X, op=ALU.add))
            link(dve.tensor_scalar(flag[:, :], count[:, :], 8.5, None, ALU.is_gt))
            link(dve.tensor_reduce(worst[:, :], full[:, :, :], axis=AX_X, op=ALU.max))
            link(dve.scalar_tensor_tensor(out=flag[:, :], in0=worst[:, :], scalar=6.5, in1=flag[:, :],
                                          op0=ALU.is_ge, op1=ALU.max))
            link(dve.tensor_reduce(worst[:, :], found[:, :, :], axis=AX_X, op=ALU.max))
            link(dve.scalar_tensor_tensor(out=flag[:, :], in0=worst[:, :], scalar=float(3 * HALF), in1=flag[:, :],
                                          op0=ALU.is_ge, op1=ALU.max))
            dve.wait_ge(s_flag_ps, 1)
            link(dve.tensor_copy(totals[:, :], ps[:, 1, NB:2 * NB]))
            link(dve.tensor_tensor_scan(worst[:, :], totals[:, :], totals[:, :], 0.0, ALU.add, ALU.bypass))
            link(dve.tensor_tensor(place[:, :], worst[:, :], totals[:, :], ALU.subtract))
            link(dve.tensor_tensor(place[:, :], place[:, :], ps[:, 1, 0:NB], ALU.add))
            link(dve.scalar_tensor_tensor(out=place[:, :], in0=place[:, :], scalar=1.0, in1=flag[:, :],
                                          op0=ALU.add, op1=ALU.mult))
            assert flagged[0] == FLAG_STEPS, flagged[0]
            with dve.Fori(0, NB // 2) as i:
                for j in range(2):
                    b = 2 * i + j
                    dve.wait_ge(s_pick_ps, b + 1)
                    dve.tensor_scalar(pick[:, j, :], rank[:, :], place[:, bass.ds(b, 1)], None,
                                      ALU.is_equal).then_inc(s_pick, 1)
            dve.wait_ge(s_pick_ps, NB + 2)
            vn = [0]

            def vlink(instruction):
                vn[0] += 1
                instruction.then_inc(s_vnum, 1)
                dve.wait_ge(s_vnum, vn[0])

            vlink(dve.tensor_copy(vnum[:, 0:1], ps[:, 3, 0:1]))
            vlink(dve.tensor_scalar(vnum[:, 1:2], vnum[:, 0:1], 0.0, float(NO_ROW), ALU.is_equal, ALU.mult))
            vlink(dve.scalar_tensor_tensor(out=vrow[:, :], in0=vnum[:, 0:1], scalar=-1.0, in1=vnum[:, 1:2],
                                           op0=ALU.add, op1=ALU.add))
            dve.tensor_scalar(vnum[:, 2:3], vnum[:, 0:1], -1.0, COL2 + 1.0, ALU.mult, ALU.add).then_inc(s_vrow, 1)

            for b in (NB - 2, NB - 1):
                block_scores(b, b % 2)
                weigh_values(b, b % 2)

            dve.wait_ge(s_vrow, 1)
            for s in range(VSEG):
                dve.wait_ge(s_keys, ALL_KEYS + s + 1)
                dve.max(out=vcand[:, 8 * s:8 * s + 8], in_=ps[:, 4 + s % RING, :]).then_inc(s_cand, 1)
            dve.wait_ge(s_cand, ALL_KEYS + VSEG)
            vs = [0]

            def slink(instruction, sem=None):
                vs[0] += 1
                instruction.then_inc(s_vsearch, 1)
                dve.wait_ge(s_vsearch, vs[0])

            slink(dve.scalar_tensor_tensor(out=vclean[:, :], in0=vcand[:, :], scalar=vnum[:, 2:3], in1=vcand[:, :],
                                           op0=ALU.not_equal, op1=ALU.mult))
            slink(dve.max(out=vtop[:, 0:8], in_=vclean[:, :]))
            slink(dve.match_replace(out=vrest[:, :], in_to_replace=vtop[:, 0:8], in_values=vclean[:, :],
                                    imm_value=-1.0))
            dve.max(out=vtop[:, 8:16], in_=vrest[:, :]).then_inc(s_top, 1)
            slink(dve.tensor_scalar(vwork[:, :], vcand[:, :], vnum[:, 2:3], None, ALU.is_equal))
            slink(dve.tensor_reduce(vstat[:, 0:1], vwork[:, :], axis=AX_X, op=ALU.add))
            slink(dve.tensor_scalar(vgap[:, 0:1], vstat[:, 0:1], -1.0, 1.0, ALU.mult, ALU.add))
            slink(dve.tensor_scalar(vwork[:, :], vclean[:, :], float(N), None, ALU.is_ge))
            slink(dve.tensor_reduce(vstat[:, 1:2], vwork[:, :], axis=AX_X, op=ALU.add))
            slink(dve.tensor_reduce(vstat[:, 2:3], vcand[:, 7::8], axis=AX_X, op=ALU.max))
            slink(dve.tensor_reduce(vstat[:, 3:4], vcand[:, :], axis=AX_X, op=ALU.max))
            slink(dve.tensor_scalar(vstat[:, 4:5], vstat[:, 1:2], 16.5, None, ALU.is_gt))
            slink(dve.scalar_tensor_tensor(out=vstat[:, 4:5], in0=vstat[:, 2:3], scalar=float(N), in1=vstat[:, 4:5],
                                           op0=ALU.is_ge, op1=ALU.max))
            slink(dve.scalar_tensor_tensor(out=vstat[:, 4:5], in0=vstat[:, 3:4], scalar=float(2 * N),
                                           in1=vstat[:, 4:5], op0=ALU.is_ge, op1=ALU.max))
            slink(dve.scalar_tensor_tensor(out=vstat[:, 4:5], in0=vnum[:, 0:1], scalar=0.0, in1=vstat[:, 4:5],
                                           op0=ALU.is_gt, op1=ALU.mult))
            dve.scalar_tensor_tensor(out=vstat[:, 5:6], in0=worst[:, NB - 1:NB], scalar=P + 0.5, in1=vstat[:, 4:5],
                                     op0=ALU.is_gt, op1=ALU.max).then_inc(s_vcheck, 1)
            dve.wait_ge(s_vload, 48)
            dve.wait_ge(s_gather[0], 64 * NB + 256)
            dve.wait_ge(s_gap, 3 * NB + 1)
            scores(NB, 0, vq[:, :, :], vgap[:, :])
            weigh_values(NB, 0)
            dve.wait_ge(s_vcheck_ps, 1)
            dve.tensor_scalar(dense_flag[:, :], ps[:, 3, 64:65], -1.0 if force_dense else 0.5, None,
                              ALU.is_gt).then_inc(s_dense, 1)

            with where_dense(dve):
                dve.memset(smax[:, 0:1], 0.0).then_inc(d_adj_free, 1)
                with dve.Fori(0, NB) as b:
                    dve.wait_ge(d_adj, 16 * b + 16)
                    dve.tensor_scalar(bias, adj_sb[:, 0, :], 0.0, NEG, ALU.is_equal, ALU.mult).then_inc(d_bias, 1)
                    dve.wait_ge(d_bias, b + 1)
                    dve.memset(smax[:, 0:1], 0.0).then_inc(d_adj_free, 1)
                    dve.wait_ge(d_qT, b + 1)
                    dve.nop(nofuse=True)
                    with dve.Fori(0, H) as h:
                        t = H * b + h + 1
                        dve.tensor_scalar(xnT[:, 1, 0:P], xnT[:, 0, 0:P], head_cols[:, bass.ds(h, 1)], None,
                                          ALU.mult).then_inc(d_qh, 1)
                        dve.wait_ge(d_s_ps, t)
                        dve.tensor_tensor(s_all, ps[:, :, :].rearrange("p a m -> p (a m)"), bias,
                                          ALU.add).then_inc(d_s, 1)
                        dve.wait_ge(d_s, t)
                        dve.tensor_reduce(smax[:, 0:1], s_all, axis=AX_X, op=ALU.max).then_inc(d_max, 1)
                        dve.wait_ge(d_max, t)
                        dve.tensor_scalar(smax[:, 1:2], smax[:, 0:1], -SCALE, None, ALU.mult).then_inc(d_neg, 1)
                        dve.wait_ge(d_exp, t)
                        dve.reciprocal(rden[:, 0:1], den[:, 0:1]).then_inc(d_rden, 1)
                        for c in range(TURNS):
                            dve.wait_ge(d_pT_ps, TURNS * (t - 1) + c + 1)
                            dve.tensor_copy(pT[:, c % 2, :], ps[:, c % 2, :]).then_inc(d_pT, 1)
                        dve.wait_ge(d_o_ps, t)
                        dve.wait_ge(d_rden, t)
                        dve.tensor_scalar(att[:, bass.ts(h, DH)], ps[:, 7, 0:DH], rden[:, 0:1], None,
                                          ALU.mult).then_inc(d_o, 1)
                dve.wait_ge(d_x2, NB)

            statistics(1, NB + 1)

            def keep_h(g, r):
                dve.wait_ge(s_xnT_ps, NB + 4 * g + r + 1)
                if r == 0:
                    wait_past(dve, s_u_ps, FC * g)
                dve.tensor_scalar(xnT[:, 0, bass.ts(r, P)], ps[:, r % 2, 0:P], ln_cols[:, 2:3],
                                  ln_cols[:, 3:4], ALU.mult, ALU.add).then_inc(s_xnT, 1)

            def keep_result(g, r, jj):
                dve.wait_ge(s_ff, 4 * g + r + 1)
                dve.tensor_copy(res[:, jj, r, :], ps[:, 2 + r % 2, 0:D]).then_inc(s_res, 1)

            def group(g, jj, i):
                for r in range(4):
                    keep_h(g, r)
                wait_past(dve, s_out[jj], 16 * i)
                for r in range(4):
                    keep_result(g, r, jj)

            group(0, 0, 0)
            group(1, 1, 0)
            with dve.Fori(1, NB // 8) as i:
                for jj in range(2):
                    group(2 * i + jj, jj, i)
            keep_h(NB // 4, 0)
            dve.wait_ge(s_out[0], 16 * (NB // 8))
            keep_result(NB // 4, 0, 0)

        @block.tensor
        def _(pe):
            pe.wait_ge(s_const, NCONST)
            pe.wait_ge(s_weights, 16 * NWEIGHTS)

            def transpose_rows(b, j, base=0):
                pe.wait_ge(s_xn, base + b + 1)
                pe.transpose(ps[:, j, 0:P], xn[:, j, :], ident[:, :]).then_inc(s_xnT_ps, 1)

            def project_qkv(b, j):
                pe.wait_ge(s_xnT, b + 1)
                wait_past(pe, s_q, b - 1)
                wait_past(pe, s_kv, b - 1)
                pe.matmul(ps[:, 2 + j, 0:D], xnT[:, j, 0:P], wqkv_sb[:, 0:D], start=True, stop=True)
                pe.matmul(ps[:, 6 + j, 0:2 * D], xnT[:, j, 0:P], wqkv_sb[:, D:3 * D], start=True,
                          stop=True).then_inc(s_qkv_ps, 1)

            transpose_rows(0, 0)
            transpose_rows(1, 1)
            project_qkv(0, 0)
            with pe.Fori(1, NB // 2) as i:
                for j in range(2):
                    b = 2 * i + j
                    pe.wait_ge(s_xnT, b - 1)
                    transpose_rows(b, j)
                    project_qkv(b - 1, 1 - j)
            project_qkv(NB - 1, 1)

            def keys(b, j):
                pe.wait_ge(s_mask, b + 1)
                for s in range(NSEG):
                    wait_past(pe, s_cand, NSEG * b + s - RING + 1)
                    low, high = slice(SEG * s, SEG * (s + 1)), slice(HALF + SEG * s, HALF + SEG * (s + 1))
                    bank = ps[:, 4 + s % RING, :]
                    pe.matmul(bank, ident_2[:, :], mask[:, j, low], start=True, stop=False)
                    pe.matmul(bank, ident_1[:, :], mask[:, j, high], start=False, stop=False)
                    pe.matmul(bank, ones33[:, :], column_key[:, high], start=False, stop=True).then_inc(s_keys, 1)

            def attention_out(b, j, n=S1):
                wait_past(pe, s_oT, b)
                pe.wait_ge(s_pv, b + 1)
                for s in range(n):
                    last = pe.matmul(ps[:, 0, 0:P], pv[j][:, s, :], ident[:, :], start=(s == 0), stop=(s == n - 1))
                last.then_inc(s_oT_ps, 1)
                wait_past(pe, s_x2, b)
                pe.matmul(ps[:, 2, 0:D], ident[:, :], block_of(xs, b), start=True, stop=False)
                pe.matmul(ps[:, 2, 0:D], ones[0:1, :], bproj_row[:, :], start=False, stop=False)
                pe.wait_ge(s_oT, b + 1)
                pe.matmul(ps[:, 2, 0:D], oT[:, j, :], wproj_sb[:, :], start=False, stop=True).then_inc(s_x2_ps, 1)

            pe.wait_ge(s_xnT, NB)
            pe.wait_ge(s_q, NB)
            pe.wait_ge(s_kv, NB)
            keys(0, 0)
            keys(1, 1)
            keys(2, 0)
            keys(3, 1)
            attention_out(0, 0)
            with pe.Fori(2, NB // 2) as i:
                for j in range(2):
                    b = 2 * i + j
                    keys(b, j)
                    attention_out(b - 3, 1 - j)

            pe.wait_ge(s_flag, 9)
            pe.matmul(ps[:, 1, 0:NB], before[:, :], flag[:, :], start=True, stop=True)
            pe.matmul(ps[:, 1, NB:2 * NB], ones[:, :], flag[:, :], start=True, stop=True).then_inc(s_flag_ps, 1)
            pe.wait_ge(s_flag, FLAG_STEPS)
            pe.matmul(ps[:, 3, 0:1], ident[:, :], before[:, 0:1], start=True, stop=True).then_inc(s_pick_ps, 2)
            with pe.Fori(0, NB // 2) as i:
                for j in range(2):
                    b = 2 * i + j
                    pe.wait_ge(s_pick, b + 1)
                    pe.matmul(ps[:, 3, 0:1], pick[:, j, :], row_number[:, bass.ds(b, 1)], start=False,
                              stop=True, skip_group_check=True).then_inc(s_pick_ps, 1)
            for b in (NB - 3, NB - 2, NB - 1):
                attention_out(b, b % 2)

            pe.wait_ge(s_mask, NB + 1)
            for s in range(VSEG):
                pe.wait_ge(s_cand, ALL_KEYS + s - RING + 1)
                cols = slice(SEG * s, SEG * (s + 1))
                pe.matmul(ps[:, 4 + s % RING, :], ident_2[:, :], mask[:, 0, cols], start=True, stop=False)
                pe.matmul(ps[:, 4 + s % RING, :], ones33[:, :], column_key[:, cols], start=False,
                          stop=True).then_inc(s_keys, 1)
            attention_out(NB, 0, S2)
            pe.wait_ge(s_vcheck, 1)
            pe.matmul(ps[:, 3, 64:65], ones[:, :], vstat[:, 5:6], start=True, stop=True).then_inc(s_vcheck_ps, 1)

            with where_dense(pe):
                with pe.Fori(0, NB) as c:
                    pe.wait_ge(d_copied, c + 1)
                    pe.transpose(ps[:, 0, 0:P], xn[:, 0, :], ident[:, :]).then_inc(d_kT_ps, 1)
                pe.wait_ge(d_kT, NB)
                pe.wait_ge(d_x, 16)
                with pe.Fori(0, NB) as b:
                    pe.wait_ge(d_q, b + 1)
                    pe.transpose(ps[:, 1, 0:P], xn[:, 1, :], ident[:, :]).then_inc(d_qT_ps, 1)
                    with pe.Fori(0, H) as h:
                        t = H * b + h + 1
                        pe.wait_ge(d_qh, t)
                        for c in range(TURNS):
                            last = pe.matmul(ps[:, c, :], xnT[:, 1, 0:P], kT[:, bass.ts(c, 512)], start=True, stop=True)
                        last.then_inc(d_s_ps, 1)
                        pe.wait_ge(d_exp, t)
                        for c in range(TURNS + 1):
                            if c < TURNS:
                                pe.wait_ge(d_pT, TURNS * (t - 1) + c - 1) if c >= 2 else None
                                for r in range(4):
                                    last = pe.transpose(ps[:, c % 2, bass.ts(r, P)],
                                                        s_all[:, bass.ts(4 * c + r, P)], ident[:, :])
                                last.then_inc(d_pT_ps, 1)
                            if c >= 1:
                                pe.wait_ge(d_pT, TURNS * (t - 1) + c)
                                for r in range(4):
                                    k = 4 * (c - 1) + r
                                    last = pe.matmul(ps[:, 7, 0:DH], pT[:, (c - 1) % 2, bass.ts(r, P)],
                                                     v_all[:, k, bass.ts(h, DH)], start=(k == 0), stop=(k == NB - 1))
                        last.then_inc(d_o_ps, 1)
                    pe.wait_ge(d_o, H * b + H)
                    pe.transpose(ps[:, 0, 0:P], att, ident[:, :]).then_inc(d_oT_ps, 1)
                    pe.matmul(ps[:, 2, 0:D], ident[:, :], block_of(xs, b), start=True, stop=False)
                    pe.matmul(ps[:, 2, 0:D], ones[0:1, :], bproj_row[:, :], start=False, stop=False)
                    pe.wait_ge(d_oT, b + 1)
                    pe.matmul(ps[:, 2, 0:D], oT[:, 0, :], wproj_sb[:, :], start=False, stop=True).then_inc(d_x2_ps, 1)
                pe.wait_ge(d_x2, NB)

            def group(g, width):
                for r in range(width):
                    pe.wait_ge(s_xnT, NB + 4 * g + r - 1)
                    transpose_rows(4 * g + r, r % 2, base=NB)
                pe.wait_ge(s_xnT, NB + 4 * g + width)
                for c in range(FC):
                    wait_past(pe, s_g, FC * g)
                    pe.matmul(ps[:, 4 + c, 0:width * P], w1_sb[:, bass.ts(c, P)], xnT[:, 0, 0:width * P],
                              start=True, stop=True).then_inc(s_u_ps, 1)
                pe.wait_ge(s_g, FC * g + FC)
                for r in range(width):
                    b = 4 * g + r
                    wait_past(pe, s_res, 4 * g if r < 2 else b - 1)
                    bank = ps[:, 2 + r % 2, 0:D]
                    for c in range(FC):
                        pe.matmul(bank, gT[:, c, bass.ts(r, P)], w2_sb[:, c, :], start=(c == 0), stop=False)
                    pe.matmul(bank, ones[0:1, :], b2_row[:, :], start=False, stop=False)
                    pe.matmul(bank, ident[:, :], block_of(xs, b), start=False, stop=True).then_inc(s_ff, 1)

            group(0, 4)
            with pe.Fori(1, NB // 4) as g:
                group(g, 4)
            group(NB // 4, 1)
_INS = ["x", "adj", "L0_gnn_w_qkv", "L0_gnn_w_proj", "L0_gnn_b_proj", "L0_gnn_w1", "L0_gnn_b1", "L0_gnn_w2",
        "L0_gnn_b2", "L0_gnn_g1", "L0_gnn_be1", "L0_gnn_g2", "L0_gnn_be2"]


def kernel(**inputs):
    import numpy as _np
    import concourse.bacc as _bacc
    from concourse import mybir as _mybir
    from concourse.bass_utils import run_bass_kernel_spmd as _run

    nc = _bacc.Bacc("TRN2", target_bir_lowering=False, num_devices=1)
    arrays, args = {}, []
    for name in _INS:
        a = _np.ascontiguousarray(inputs[name])
        arrays[f"in_{name}"] = a
        args.append(nc.dram_tensor(f"in_{name}", a.shape, _mybir.dt.from_np(a.dtype), kind="ExternalInput").ap())
    out = nc.dram_tensor("out_rows", (N, D), F32, kind="ExternalOutput").ap()
    graph_layer(nc, *args, out)
    r = _run(nc, [arrays], core_ids=[0])
    return r.results[0]["out_rows"]
```

```python
from contextlib import ExitStack

import concourse.bass as bass
from concourse import mybir


F32 = mybir.dt.float32
BF16 = mybir.dt.bfloat16
I32 = mybir.dt.int32
U32 = mybir.dt.uint32
ALU = mybir.AluOpType
ACT = mybir.ActivationFunctionType
AX_X = mybir.AxisListType.X

P = 128
N = 4096
D = 128
H = 8
DH = D // H
FF = 512
FC = FF // P
NB = N // P
SCALE = float(DH) ** -0.5
EPS = 1e-5
NEG = -1.0e30

SEG = 512
RING = 4
G = 4
NG = NB // G
RINGS = 4
HALF = N // 2
NSEG = HALF // SEG
VSEG = N // SEG
SELF = 1
S1 = SELF + 8
S2 = SELF + 16
COL1 = float(HALF + N - 1)
COL2 = float(2 * N - 1)
NO_ROW = 2 * N


def block_of(tile, b):
    return tile[:, bass.ds(b, 1), :].rearrange("p a d -> p (a d)")


def wait_past(eng, sem, count):
    if not isinstance(count, int) or count > 0:
        eng.wait_ge(sem, count)


def over_heads(tile, slots):
    return tile.rearrange("p (s a) -> p s a", a=1).to_broadcast([P, slots, H])


def over_slots(tile, slots):
    return tile.rearrange("p (a h) -> p a h", a=1).to_broadcast([P, slots, H])


def graph_layer(nc, x, adj, w_qkv, w_proj, b_proj, w1, b1, w2, b2, g1, be1, g2, be2, out, force_dense=False):
    kv_dram = nc.dram_tensor("kv_table", [N, 2 * D], F32).ap()
    q_dram = nc.dram_tensor("q_table", [N, D], F32).ap()
    x_cols = x.rearrange("(b p) d -> p b d", p=P)
    out_rows = out.rearrange("(b p) d -> b p d", p=P)
    adj_rows = adj.rearrange("(b p) m -> b p m", p=P)
    kv_rows = kv_dram.rearrange("(b p) d -> b p d", p=P)

    ctx = ExitStack()
    with ctx:
        def sb(name, shape, dt=F32):
            return ctx.enter_context(nc.sbuf_tensor(name, shape, dt))

        def sem(name):
            return ctx.enter_context(nc.semaphore(name))

        ident = sb("ident", [P, P])
        ident_1 = sb("ident_1", [P, P], BF16)
        ident_2 = sb("ident_2", [P, P], BF16)
        ones33 = sb("ones33", [33, P], BF16)
        column_key = sb("column_key", [33, N], BF16)
        ones = sb("ones", [P, P])
        before = sb("before", [P, P])
        rank = sb("rank", [P, P])
        row_number = sb("row_number", [P, NB])
        self_key = sb("self_key", [P, NB])
        head_cols = sb("head_cols", [P, H])
        consts = sb("consts", [P, 4])
        col1, half_col, col2, n_col = (consts[:, i:i + 1] for i in range(4))
        wqkv_sb = sb("wqkv_sb", [P, 3 * D])
        wproj_sb = sb("wproj_sb", [P, D])
        w1_sb = sb("w1_sb", [P, FF])
        w2_sb = sb("w2_sb", [P, FC, D])
        bproj_row = sb("bproj_row", [1, D])
        b2_row = sb("b2_row", [1, D])
        b1_col = sb("b1_col", [P, FC])
        ln_cols = sb("ln_cols", [P, 4])
        diag = sb("diag", [P, NB], I32)

        xs = sb("xs", [P, NB + 1, D])
        qs = sb("qs", [P, NB, D])
        slots = sb("slots", [P, RINGS * S1 + S2, 2 * D])
        vq = sb("vq", [P, 1, D])
        adj_sb = sb("adj_sb", [P, 2, N], I32)
        mask = sb("mask", [P, 2, N], BF16)

        stats = sb("stats", [P, 2, G, 6])
        mean = sb("mean", [P, 2, G])
        var = sb("var", [P, 2, G])
        half = sb("half", [P, 2, G])
        rstd = sb("rstd", [P, 2, G])
        shift = sb("shift", [P, 2, G])
        xn = sb("xn", [P, 2, G, D])
        xnT = sb("xnT", [P, 2, G * P])

        cand = sb("cand", [P, NSEG * 8])
        clean = sb("clean", [P, 2, NSEG * 8])
        found = sb("found", [P, NB, NSEG * 8])
        top = sb("top", [P, 2, 8])
        gap = sb("gap", [P, RINGS, S1])
        idx = sb("idx", [P, RINGS, 8], I32)
        self_gap = sb("self_gap", [P, NB])
        vcand = sb("vcand", [P, VSEG * 8])
        vclean = sb("vclean", [P, VSEG * 8])
        vrest = sb("vrest", [P, VSEG * 8])
        vtop = sb("vtop", [P, 16])
        vgap = sb("vgap", [P, S2])
        vidx = sb("vidx", [P, 16], I32)
        flag = sb("flag", [P, NB])
        full = sb("full", [P, NB, NSEG])
        count = sb("count", [P, NB])
        worst = sb("worst", [P, NB])
        totals = sb("totals", [P, NB])
        place = sb("place", [P, NB])
        vnum = sb("vnum", [P, 4])
        vrow = sb("vrow", [P, 1], I32)
        vwork = sb("vwork", [P, VSEG * 8])
        vstat = sb("vstat", [P, 6])
        dense_flag = sb("dense_flag", [P, 1], I32)

        prod = sb("prod", [P, S2, D])
        sc = sb("sc", [P, S2, H])
        smax = sb("smax", [P, H])
        ex = sb("ex", [P, S2, H])
        den = sb("den", [P, H])
        rden = sb("rden", [P, H])
        pr = sb("pr", [P, S2, H])
        pv0 = sb("pv0", [P, S2, D])
        pv1 = sb("pv1", [P, S1, D])
        pv = (pv0, pv1)
        work = prod[:, S1:S2, :].rearrange("p s (b k) -> p (s b) k", k=NSEG * 8)
        pick = pv0[:, S1:S1 + G, :]
        oT = sb("oT", [P, 2, P])
        gT = sb("gT", [P, FC, G * P])
        res = sb("res", [P, G, D])
        ps = ctx.enter_context(nc.psum_tensor("ps", [P, 8, 512], F32))
        OUT_T, ROWS, X2, UP, KEYS = 0, 1, 2, 3, 4

        s_const = sem("s_const")
        s_weights = sem("s_weights")
        s_diag = sem("s_diag")
        s_x = [sem(f"s_x_part{i}") for i in range(4)]
        s_adj = [sem("s_adj0"), sem("s_adj1")]
        s_moments = sem("s_moments")
        s_sqrt = sem("s_sqrt")
        s_rstd = sem("s_rstd")
        s_shift = sem("s_shift")
        s_xn = sem("s_xn")
        s_xnT_ps = sem("s_xnT_ps")
        s_xnT = sem("s_xnT")
        s_q_ps = sem("s_q_ps")
        s_kv_ps = sem("s_kv_ps")
        s_q = sem("s_q")
        s_kv = sem("s_kv")
        s_kv_stored = sem("s_kv_stored")
        s_q_stored = sem("s_q_stored")
        s_self = [sem(f"s_self{i}") for i in range(RINGS)]
        s_mask = sem("s_mask")
        s_keys = sem("s_keys")
        s_cand = sem("s_cand")
        s_clean = sem("s_clean")
        s_top = sem("s_top")
        s_idx = sem("s_idx")
        s_gap = sem("s_gap")
        s_gather = [sem(f"s_gather{i}") for i in range(RINGS)]
        s_flag = sem("s_flag")
        s_flag_ps = sem("s_flag_ps")
        s_pick = sem("s_pick")
        s_pick_ps = sem("s_pick_ps")
        s_vnum = sem("s_vnum")
        s_vrow = sem("s_vrow")
        s_vadj = sem("s_vadj")
        s_vload = sem("s_vload")
        s_vsearch = sem("s_vsearch")
        s_vcheck = sem("s_vcheck")
        s_vcheck_ps = sem("s_vcheck_ps")
        s_vgather = sem("s_vgather")
        s_dense = sem("s_dense")
        s_score = sem("s_score")
        s_exp = sem("s_exp")
        s_soft = sem("s_soft")
        s_pv = sem("s_pv")
        s_oT_ps = sem("s_oT_ps")
        s_oT = sem("s_oT")
        s_x2_ps = sem("s_x2_ps")
        s_x2 = sem("s_x2")
        s_u_ps = sem("s_u_ps")
        s_g = sem("s_g")
        s_ff = sem("s_ff")
        s_res = sem("s_res")
        s_out = sem("s_out")
        s_vout = sem("s_vout")

        d_load = sem("d_load")
        d_copied = sem("d_copied")
        d_kT_ps = sem("d_kT_ps")
        d_kT = sem("d_kT")
        d_x = sem("d_x")
        d_adj_free = sem("d_adj_free")
        d_adj = sem("d_adj")
        d_bias = sem("d_bias")
        d_q = sem("d_q")
        d_qT_ps = sem("d_qT_ps")
        d_qT = sem("d_qT")
        d_qh = sem("d_qh")
        d_s_ps = sem("d_s_ps")
        d_s = sem("d_s")
        d_max = sem("d_max")
        d_neg = sem("d_neg")
        d_exp = sem("d_exp")
        d_rden = sem("d_rden")
        d_pT_ps = sem("d_pT_ps")
        d_pT = sem("d_pT")
        d_o_ps = sem("d_o_ps")
        d_o = sem("d_o")
        d_oT_ps = sem("d_oT_ps")
        d_oT = sem("d_oT")
        d_x2_ps = sem("d_x2_ps")
        d_x2 = sem("d_x2")

        kT = slots[:, 0:16, :].rearrange("p s d -> p (s d)")
        v_all = slots[:, 16:32, :].rearrange("p s (a d) -> p (s a) d", a=2)
        bias = adj_sb[:, 1, :].bitcast(F32)
        s_all = mask[:, :, :].rearrange("p a m -> p (a m)").bitcast(F32)
        pT = gT[:, 0:2, :]
        att = prod[:, 0, :]
        TURNS = 8

        block = ctx.enter_context(nc.Block())

        def where_dense(eng):
            eng.wait_ge(s_dense, 1)
            eng.wait_ge(s_res, NG + 1)
            return eng.If(eng.value_load(dense_flag[0:1, 0:1], min_val=0, max_val=1) > 0)

        NWEIGHTS = 11
        NCONST = 24
        IDENT_MADE = 2
        SCORE_STEPS = 5
        FLAG_STEPS = 14
        ALL_KEYS = NSEG * NB
        LN_B, LN_V, LN_D = NG, 2 * NG, 2 * NG + 1
        FF_V, FF_D = NG, NG + 1

        def slot_tile(b, r):
            if isinstance(b, int) and b == NB:
                return slots[:, RINGS * S1:RINGS * S1 + S2, :], S2
            return slots[:, S1 * r:S1 * (r + 1), :], S1

        def ring_count(b, r, per):
            if isinstance(b, int):
                return per * (b // RINGS + 1)
            return (per // RINGS) * (b - r) + per

        def blocks_of(tile, g, width=None):
            if width is not None and width != G:
                return tile[:, NB:NB + width, :]
            return tile[:, bass.ts(g, G), :]

        @block.sync
        def _(sp):
            for c in range(4):
                w = NB // 4
                sp.dma_start(xs[:, w * c:w * (c + 1), :], x_cols[:, w * c:w * (c + 1), :]).then_inc(s_x[c], 16)
            sp.dma_start(adj_sb[:, 0, :], adj_rows[0, :, :]).then_inc(s_adj[0], 16)
            sp.dma_start(adj_sb[:, 1, :], adj_rows[1, :, :]).then_inc(s_adj[1], 16)
            for c in range(NG // 2):
                sp.wait_ge(s_kv, 2 * c + 2)
                w = 2 * G
                sp.dma_start(kv_rows[w * c:w * (c + 1), :, :].rearrange("b p d -> p b d"),
                             slots[:, w * c:w * (c + 1), :]).then_inc(s_kv_stored, 16)
            sp.wait_ge(s_q, NG)
            sp.dma_start(q_dram.rearrange("(b p) d -> p b d", p=P), qs[:, :, :]).then_inc(s_q_stored, 16)
            sp.wait_ge(s_kv_stored, 16 * (NG // 2))
            for b in range(3):
                sp.dma_start(slots[:, S1 * b, :], kv_rows[b, :, :]).then_inc(s_self[b], 16)

            def turn(s, r):
                b = s + 2
                if not isinstance(s, int) or b < NB:
                    sp.wait_ge(s_mask, b - 1)
                    sp.dma_start(adj_sb[:, r % 2, :], adj_rows[b, :, :]).then_inc(s_adj[r % 2], 16)
                b = s - 2
                if not isinstance(s, int) or 3 <= b < NB:
                    wait_past(sp, s_pv, b - RINGS + 1)
                    at = (r - 2) % RINGS
                    sp.dma_start(slots[:, S1 * at, :], kv_rows[b, :, :]).then_inc(s_self[at], 16)

            def store(g):
                sp.wait_ge(s_res, g + 1)
                sp.dma_start(out_rows[bass.ts(g, G), :, :].rearrange("b p d -> p b d"), res[:, :, :]).then_inc(s_out, 16)

            for g in range(4):
                for r in range(G):
                    turn(G * g + r, r)
            with sp.Fori(4, NG - 1) as g:
                for r in range(G):
                    turn(G * g + r, r)
                    if r == 1:
                        store(g - 4)
            for g in (NG - 1, NG):
                for r in range(G):
                    turn(G * g + r, r)
                    if r == 1:
                        store(g - 4)
            for g in range(NG - 3, NG):
                store(g)
            sp.wait_ge(s_out, 16 * NG)

            with where_dense(sp):
                kv_cols = kv_dram.rearrange("(b p) d -> p b d", p=P)
                sp.wait_ge(s_vout, 16)
                sp.dma_start(xs[:, 0:NB, :], kv_cols[:, :, 0:D]).then_inc(d_load, 16)
                sp.dma_start(v_all, kv_cols[:, :, D:2 * D]).then_inc(d_load, 16)
                sp.wait_ge(d_copied, NB)
                sp.dma_start(xs[:, 0:NB, :], x_cols).then_inc(d_x, 16)
                with sp.Fori(0, NB) as b:
                    sp.wait_ge(d_adj_free, b + 1)
                    sp.dma_start(adj_sb[:, 0, :], adj_rows[b, :, :]).then_inc(d_adj, 16)
                with sp.Fori(0, NG) as g:
                    sp.wait_ge(s_res, FF_D + g + 1)
                    sp.dma_start(out_rows[bass.ts(g, G), :, :].rearrange("b p d -> p b d"),
                                 res[:, :, :]).then_inc(s_out, 16)
                sp.wait_ge(s_out, 32 * NG)

        @block.gpsimd
        def _(pool):
            made = [0]

            def step(instruction):
                made[0] += 1
                instruction.then_inc(s_const, 1)
                pool.wait_ge(s_const, made[0])

            step(pool.memset(ident[:, :], 0.0))
            step(pool.affine_select(out=ident[:, :], in_=ident[:, :], compare_op=ALU.not_equal, fill=1.0,
                                    base=0, pattern=[[-1, P]], channel_multiplier=1))
            assert made[0] == IDENT_MADE
            for tile, value in ((ident_1, float(HALF)), (ident_2, float(N))):
                step(pool.memset(tile[:, :], 0.0))
                step(pool.affine_select(out=tile[:, :], in_=tile[:, :], compare_op=ALU.not_equal, fill=value,
                                        base=0, pattern=[[-1, P]], channel_multiplier=1))
            step(pool.memset(ones33[:, :], 1.0))
            step(pool.memset(ones[:, :], 1.0))
            for col, value in ((col1, COL1), (half_col, float(HALF)), (col2, COL2), (n_col, float(N))):
                step(pool.memset(col, value))
            step(pool.memset(column_key[:, :], 0.0))
            step(pool.iota(column_key[0:1, :], pattern=[[-64, N // 64], [0, 64]], base=N - 64, channel_multiplier=0,
                           allow_small_or_imprecise_dtypes=True))
            step(pool.iota(column_key[32:33, :], pattern=[[0, N // 64], [-1, 64]], base=63, channel_multiplier=0,
                           allow_small_or_imprecise_dtypes=True))
            step(pool.iota(self_key[:, :], pattern=[[-P, NB]], base=int(COL1), channel_multiplier=-1,
                           allow_small_or_imprecise_dtypes=True))
            step(pool.memset(slots[:, NB:RINGS * S1 + S2, :], 0.0))
            step(pool.affine_select(out=before[:, :], in_=ones[:, :], compare_op=ALU.is_gt, fill=0.0,
                                    base=0, pattern=[[1, P]], channel_multiplier=-1))
            step(pool.iota(rank[:, :], pattern=[[1, P]], base=1, channel_multiplier=0,
                           allow_small_or_imprecise_dtypes=True))
            step(pool.iota(row_number[:, :], pattern=[[P, NB]], base=1, channel_multiplier=1,
                           allow_small_or_imprecise_dtypes=True))
            step(pool.affine_select(out=head_cols[:, :], in_=ones[:, 0:H], compare_op=ALU.is_ge, fill=0.0,
                                    base=0, pattern=[[-DH, H]], channel_multiplier=1))
            step(pool.affine_select(out=head_cols[:, :], in_=head_cols[:, :], compare_op=ALU.is_ge, fill=0.0,
                                    base=DH - 1, pattern=[[DH, H]], channel_multiplier=-1))
            step(pool.memset(xs[:, NB, :], 0.0))
            step(pool.memset(vq[:, 0, :], 0.0))
            assert made[0] == NCONST, made[0]

            def gather_rows(dst, table, row, sem):
                pool.indirect_dma_start(out=dst, out_offset=None, in_=table,
                                        in_offset=bass.IndirectOffsetOnAxis(ap=row.bitcast(U32), axis=0),
                                        bounds_check=N - 1, oob_is_err=False).then_inc(sem, 16)

            def gather(b, r):
                pool.wait_ge(s_idx, b + 1)
                wait_past(pool, s_pv, b - RINGS + 1)
                pool.nop(nofuse=True)
                for s in range(8):
                    gather_rows(slots[:, S1 * r + SELF + s, :], kv_dram[:, :], idx[:, r, s:s + 1], s_gather[r])

            pool.wait_ge(s_kv_stored, 16 * (NG // 2))
            for b in range(G):
                gather(b, b)
            with pool.Fori(1, NG - 1) as g:
                for r in range(G):
                    gather(G * g + r, r)
            for b in range(NB - G, NB - 1):
                gather(b, b % G)

            pool.wait_ge(s_vrow, 1)
            pool.wait_ge(s_mask, NB)
            pool.wait_ge(s_q_stored, 16)
            gather_rows(adj_sb[:, 0, :], adj[:, :], vrow[:, 0:1], s_vadj)
            gather(NB - 1, G - 1)
            gather_rows(slots[:, RINGS * S1, :], kv_dram[:, :], vrow[:, 0:1], s_vload)
            gather_rows(vq[:, 0, :], q_dram[:, :], vrow[:, 0:1], s_vload)
            gather_rows(xs[:, NB, :], x[:, :], vrow[:, 0:1], s_vload)
            pool.wait_ge(s_idx, NB + 1)
            for s in range(16):
                gather_rows(slots[:, RINGS * S1 + SELF + s, :], kv_dram[:, :], vidx[:, s:s + 1], s_vgather)

            pool.wait_ge(s_out, 16 * NG)
            pool.wait_ge(s_res, NG + 1)
            pool.indirect_dma_start(out=out[:, :], out_offset=bass.IndirectOffsetOnAxis(
                ap=vrow[:, 0:1].bitcast(U32), axis=0), in_=res[:, 0, :], in_offset=None,
                bounds_check=N - 1, oob_is_err=False).then_inc(s_vout, 16)
            pool.wait_ge(s_vout, 16)

        @block.scalar
        def _(act):
            for dst, src in ((ln_cols[:, 0:1], g1.rearrange("(p a) -> p a", a=1)),
                             (ln_cols[:, 1:2], be1.rearrange("(p a) -> p a", a=1)),
                             (wqkv_sb[:, :], w_qkv), (wproj_sb[:, :], w_proj), (w1_sb[:, :], w1),
                             (w2_sb[:, :, :], w2.rearrange("(c p) n -> p c n", p=P)),
                             (bproj_row[:, :], b_proj.rearrange("(a n) -> a n", a=1)),
                             (b2_row[:, :], b2.rearrange("(a n) -> a n", a=1)),
                             (b1_col[:, :], b1.rearrange("(c p) -> p c", p=P)),
                             (ln_cols[:, 2:3], g2.rearrange("(p a) -> p a", a=1)),
                             (ln_cols[:, 3:4], be2.rearrange("(p a) -> p a", a=1))):
                act.dma_start(dst, src, allow_slow_non_contiguous=True).then_inc(s_weights, 16)
            act.dma_start(diag[:, :], bass.AP(tensor=adj.tensor, offset=0, ap=[[N + 1, P], [P * (N + 1), NB]]),
                          allow_slow_non_contiguous=True).then_inc(s_diag, 16)

            def deviation(k, j=0, before=1):
                act.wait_ge(s_moments, 7 * k + 7)
                wait_past(act, s_xn, k - before + 1)
                act.activation(rstd[:, j, :], var[:, j, :], ACT.Sqrt).then_inc(s_sqrt, 1)

            def keep_rows_T(k, bank, norm, j=0, width=G):
                act.wait_ge(s_xnT_ps, k + 1)
                w = width * P
                act.activation(xnT[:, j, 0:w], ps[:, bank, 0:w], ACT.Identity, scale=ln_cols[:, 2 * norm:2 * norm + 1],
                               bias=ln_cols[:, 2 * norm + 1:2 * norm + 2]).then_inc(s_xnT, 1)

            def make_mask(b, j):
                act.wait_ge(s_adj[j], 8 * (b - j) + 16)
                wait_past(act, s_keys, NSEG * (b - 1))
                act.activation(mask[:, j, :], adj_sb[:, j, :], ACT.Square).then_inc(s_mask, 1)

            act.wait_ge(s_weights, 16 * NWEIGHTS)
            for k in range(NG + 3):
                if k < NG:
                    deviation(k, k % 2, 2)
                if 1 <= k <= NG:
                    wait_past(act, s_kv_ps, k - 2)
                    keep_rows_T(k - 1, 4 * ((k - 1) % 2), 0, (k - 1) % 2)
                if k >= 3:
                    act.wait_ge(s_q_ps, k - 2)
                    act.activation(qs[:, G * (k - 3):G * (k - 2), :].rearrange("p b d -> p (b d)"),
                                   ps[:, 4 * ((k - 3) % 2) + 1, :], ACT.Copy).then_inc(s_q, 1)
                if k == NG // 2:
                    make_mask(0, 0)

            act.wait_ge(s_const, NCONST)
            act.wait_ge(s_flag, 1)

            def slot_numbers(b, r):
                j = r % 2
                act.wait_ge(s_top, b + 1)
                wait_past(act, s_gather[r], ring_count(b, r, 128) - 128)
                act.activation(idx[:, r, :], top[:, j, :], ACT.Relu, scale=-1.0, bias=col1).then_inc(s_idx, 1)
                wait_past(act, s_score, SCORE_STEPS * (b - RINGS + 1))
                act.activation(gap[:, r, SELF:S1], top[:, j, :], ACT.Relu, scale=-1.0, bias=half_col).then_inc(s_gap, 1)
                act.activation(gap[:, r, 0:1], self_gap[:, bass.ds(b, 1)], ACT.Copy).then_inc(s_gap, 1)
                act.activation(block_of(found, b), clean[:, j, :], ACT.Copy).then_inc(s_gap, 1)

            def exponentials(b, n=S1):
                act.wait_ge(s_score, SCORE_STEPS * (b + 1))
                wait_past(act, s_soft, 3 * b)
                act.activation(ex[:, 0:n, :], sc[:, 0:n, :], ACT.Exp, scale=SCALE).then_inc(s_exp, 1)

            def attention_out(b, j):
                act.wait_ge(s_oT_ps, b + 1)
                act.activation(oT[:, j, :], ps[:, OUT_T, 0:P], ACT.Copy).then_inc(s_oT, 1)
                act.wait_ge(s_x2_ps, b + 1)
                act.activation(block_of(xs, b), ps[:, X2, 0:D], ACT.Copy).then_inc(s_x2, 1)

            def gelu_up(kf, width=G):
                w = width * P
                for c in range(FC):
                    act.wait_ge(s_u_ps, FC * kf + c + 1)
                    wait_past(act, s_ff, kf)
                    act.activation(gT[:, c, 0:w], ps[:, (UP, ROWS)[c % 2], 0:w], ACT.Gelu_apprx_tanh,
                                   bias=b1_col[:, c:c + 1]).then_inc(s_g, 1)

            def keep_result(kf, width=G, stored=None):
                act.wait_ge(s_ff, kf + 1)
                wait_past(act, s_out, 16 * kf if stored is None else stored)
                act.activation(res[:, 0:width, :].rearrange("p b d -> p (b d)"), ps[:, UP, 0:width * D],
                               ACT.Copy).then_inc(s_res, 1)

            def turn(s, r, g):
                static = isinstance(s, int)
                if not static or s + 1 < NB:
                    make_mask(s + 1, (r + 1) % 2)
                if not static or 4 <= s < NB + 4:
                    exponentials(s - 4)
                if not static or s < NB:
                    slot_numbers(s, r)
                if not static or 5 <= s < NB + 5:
                    attention_out(s - 5, (r + 1) % 2)
                if r == 2 and (not static or g >= 3):
                    gelu_up(g - 3)
                if r == 2 and (not static or g >= 2):
                    deviation(LN_B + g - 2)
                if r == 3 and (not static or g >= 3):
                    keep_result(g - 3)
                if r == 3 and (not static or g >= 2):
                    keep_rows_T(LN_B + g - 2, ROWS, 1)

            for g in range(4):
                for r in range(G):
                    turn(G * g + r, r, g)
            with act.Fori(4, NG - 1) as g:
                for r in range(G):
                    turn(G * g + r, r, g)
            for r in range(G):
                turn(NB - G + r, r, NG - 1)
            for r in range(G - 1):
                turn(NB + r, r, NG)
            act.wait_ge(s_vadj, 16)
            act.activation(mask[:, 0, :], adj_sb[:, 0, :], ACT.Square).then_inc(s_mask, 1)
            act.wait_ge(s_top, NB + 1)
            act.activation(vidx[:, :], vtop[:, :], ACT.Relu, scale=-1.0, bias=col2).then_inc(s_idx, 1)
            act.activation(vgap[:, SELF:S2], vtop[:, :], ACT.Relu, scale=-1.0, bias=n_col).then_inc(s_gap, 1)
            turn(NB + G - 1, G - 1, NG)
            attention_out(NB - 1, 1)
            gelu_up(NG - 2)
            deviation(LN_B + NG - 1)
            keep_result(NG - 2)
            keep_rows_T(LN_B + NG - 1, ROWS, 1)
            gelu_up(NG - 1)
            keep_result(NG - 1)
            exponentials(NB, S2)
            attention_out(NB, 0)
            deviation(LN_V)
            keep_rows_T(LN_V, ROWS, 1, width=1)
            gelu_up(FF_V, 1)
            keep_result(FF_V, 1)

            with where_dense(act):
                act.wait_ge(d_load, 32)
                with act.Fori(0, NB) as c:
                    act.activation(xn[:, 0, 0, :], block_of(xs, c), ACT.Copy).then_inc(d_copied, 1)
                    act.wait_ge(d_kT_ps, c + 1)
                    act.activation(kT[:, bass.ts(c, P)], ps[:, 0, 0:P], ACT.Copy).then_inc(d_kT, 1)
                with act.Fori(0, NB) as b:
                    act.activation(xn[:, 1, 0, :], block_of(qs, b), ACT.Copy).then_inc(d_q, 1)
                    act.wait_ge(d_qT_ps, b + 1)
                    act.activation(xnT[:, 0, 0:P], ps[:, 1, 0:P], ACT.Copy).then_inc(d_qT, 1)
                    with act.Fori(0, H) as h:
                        act.wait_ge(d_neg, H * b + h + 1)
                        act.activation(s_all, s_all, ACT.Exp, scale=SCALE, bias=smax[:, 1:2],
                                       accum_out=den[:, 0:1]).then_inc(d_exp, 1)
                    act.wait_ge(d_oT_ps, b + 1)
                    act.activation(oT[:, 0, :], ps[:, 0, 0:P], ACT.Copy).then_inc(d_oT, 1)
                    act.wait_ge(d_x2_ps, b + 1)
                    act.activation(block_of(xs, b), ps[:, 2, 0:D], ACT.Copy).then_inc(d_x2, 1)
                with act.Fori(0, NG) as g:
                    deviation(LN_D + g)
                    keep_rows_T(LN_D + g, ROWS, 1)
                    gelu_up(FF_D + g)
                    act.wait_ge(s_vout, 16)
                    keep_result(FF_D + g, stored=16 * (FF_D + g) - 16)

        @block.vector
        def _(dve):
            def moments(k, rows, width=G, j=0, before=1):
                for i in range(width):
                    last = dve.bn_stats(stats[:, j, i, :], rows(i))
                last.then_inc(s_moments, 1)
                dve.wait_ge(s_moments, 7 * k + 1)
                w = slice(0, width)
                even, odd = stats[:, j, w, 1], stats[:, j, w, 4]
                dve.tensor_tensor(mean[:, j, w], even, odd, ALU.add).then_inc(s_moments, 1)
                dve.tensor_tensor(half[:, j, w], even, odd, ALU.subtract).then_inc(s_moments, 1)
                wait_past(dve, s_sqrt, k - before + 1)
                dve.scalar_tensor_tensor(out=var[:, j, w], in0=stats[:, j, w, 2], scalar=EPS * D,
                                         in1=stats[:, j, w, 5], op0=ALU.add, op1=ALU.add).then_inc(s_moments, 1)
                dve.wait_ge(s_moments, 7 * k + 4)
                dve.tensor_scalar(mean[:, j, w], mean[:, j, w], -0.5, None, ALU.mult).then_inc(s_moments, 1)
                dve.scalar_tensor_tensor(out=half[:, j, w], in0=half[:, j, w], scalar=0.25, in1=half[:, j, w],
                                         op0=ALU.mult, op1=ALU.mult).then_inc(s_moments, 1)
                dve.wait_ge(s_moments, 7 * k + 6)
                dve.scalar_tensor_tensor(out=var[:, j, w], in0=var[:, j, w], scalar=1.0 / D, in1=half[:, j, w],
                                         op0=ALU.mult, op1=ALU.add).then_inc(s_moments, 1)

            def scale_rows(k, j=0):
                dve.wait_ge(s_sqrt, k + 1)
                dve.reciprocal(rstd[:, j, :], rstd[:, j, :]).then_inc(s_rstd, 1)
                dve.wait_ge(s_rstd, k + 1)
                dve.tensor_tensor(shift[:, j, :], mean[:, j, :], rstd[:, j, :], ALU.mult).then_inc(s_shift, 1)

            def normalise(k, rows, width=G, j=0, before=1):
                dve.wait_ge(s_shift, k + 1)
                wait_past(dve, s_xnT_ps, k - before + 1)
                for i in range(width):
                    last = dve.tensor_scalar(xn[:, j, i, :], rows(i), rstd[:, j, i:i + 1], shift[:, j, i:i + 1],
                                             ALU.mult, ALU.add)
                last.then_inc(s_xn, 1)

            for tile in (var, mean, rstd, half, shift):
                dve.memset(tile[:, :, :], 1.0)

            def input_rows(k):
                return lambda i: xs[:, G * k + i, :]

            for k in range(NG + 3):
                if k < NG:
                    dve.wait_ge(s_x[k // 2], 16)
                    moments(k, input_rows(k), j=k % 2, before=2)
                if 1 <= k <= NG:
                    scale_rows(k - 1, (k - 1) % 2)
                    normalise(k - 1, input_rows(k - 1), j=(k - 1) % 2, before=2)
                if k >= 3:
                    c, bank = k - 3, 4 * ((k - 3) % 2) + 2
                    dve.wait_ge(s_kv_ps, c + 1)
                    dve.tensor_copy(slots[:, G * c:G * (c + 1), :].rearrange("p b d -> p (b d)"),
                                    ps[:, bank:bank + 2, :].rearrange("p a m -> p (a m)")).then_inc(s_kv, 1)
            dve.wait_ge(s_diag, 16)
            dve.tensor_scalar(self_gap[:, :], diag[:, :], 0.0, None, ALU.is_equal).then_inc(s_flag, 1)
            dve.wait_ge(s_q, NG)
            dve.wait_ge(s_const, NCONST)

            def group_rows(g):
                return lambda i: block_of(xs, G * g + i)

            def search(b, i):
                dve.wait_ge(s_keys, NSEG * b + i + 1)
                dve.nop(nofuse=True)
                dve.max(out=cand[:, 8 * i:8 * i + 8], in_=ps[:, KEYS + i, :]).then_inc(s_cand, 1)

            def drop_self(b, j):
                dve.wait_ge(s_cand, NSEG * (b + 1))
                wait_past(dve, s_gap, 3 * (b - 1))
                dve.scalar_tensor_tensor(out=clean[:, j, :], in0=cand[:, :], scalar=self_key[:, bass.ds(b, 1)],
                                         in1=cand[:, :], op0=ALU.not_equal, op1=ALU.mult).then_inc(s_clean, 1)

            def best(b, j):
                dve.wait_ge(s_clean, b + 1)
                dve.nop(nofuse=True)
                dve.max(out=top[:, j, :], in_=clean[:, j, :]).then_inc(s_top, 1)

            def score_steps(b, r, q, gaps):
                tile, n = slot_tile(b, r)

                def after(step):
                    dve.wait_ge(s_score, SCORE_STEPS * b + step)

                def products():
                    dve.tensor_tensor(prod[:, 0:n, :], tile[:, :, 0:D], q.to_broadcast([P, n, D]),
                                      ALU.mult).then_inc(s_score, 1)

                def head_sums():
                    after(1)
                    wait_past(dve, s_exp, b)
                    dve.tensor_reduce(sc[:, 0:n, :].rearrange("p s h -> p (s h)"),
                                      prod[:, 0:n, :].rearrange("p s (h e) -> p (s h) e", e=DH),
                                      axis=AX_X, op=ALU.add).then_inc(s_score, 1)

                def shut_empty():
                    after(2)
                    dve.scalar_tensor_tensor(out=sc[:, 0:n, :], in0=over_heads(gaps, n), scalar=NEG,
                                             in1=sc[:, 0:n, :], op0=ALU.mult, op1=ALU.add).then_inc(s_score, 1)

                def maximum():
                    after(3)
                    dve.tensor_reduce(smax[:, :], sc[:, 0:n, :].rearrange("p s h -> p h s"), axis=AX_X,
                                      op=ALU.max).then_inc(s_score, 1)

                def less_maximum():
                    after(4)
                    dve.tensor_tensor(sc[:, 0:n, :], sc[:, 0:n, :], over_slots(smax[:, :], n),
                                      ALU.subtract).then_inc(s_score, 1)

                return products, head_sums, shut_empty, maximum, less_maximum

            def block_steps(b, r):
                dve.wait_ge(s_gather[r], ring_count(b, r, 128))
                dve.wait_ge(s_self[r], ring_count(b, r, 16))
                dve.wait_ge(s_gap, 3 * (b + 1))
                return score_steps(b, r, qs[:, bass.ds(b, 1), :], gap[:, r, :])

            def denominators(b, n):
                dve.wait_ge(s_exp, b + 1)
                dve.tensor_reduce(den[:, :], ex[:, 0:n, :].rearrange("p s h -> p h s"), axis=AX_X,
                                  op=ALU.add).then_inc(s_soft, 1)

            def weigh_values(b, r, n):
                tile = slot_tile(b, r)[0]
                dve.wait_ge(s_soft, 3 * b + 1)
                dve.reciprocal(rden[:, :], den[:, :]).then_inc(s_soft, 1)
                dve.wait_ge(s_soft, 3 * b + 2)
                dve.tensor_tensor(pr[:, 0:n, :], ex[:, 0:n, :], over_slots(rden[:, :], n),
                                  ALU.mult).then_inc(s_soft, 1)
                dve.wait_ge(s_soft, 3 * b + 3)
                wait_past(dve, s_oT_ps, b - 1)
                dve.tensor_tensor(pv[r % 2][:, 0:n, :].rearrange("p s (h e) -> p s h e", e=DH),
                                  tile[:, :, D:2 * D].rearrange("p s (h e) -> p s h e", e=DH),
                                  pr[:, 0:n, :].rearrange("p s (h a) -> p s h a", a=1).to_broadcast([P, n, H, DH]),
                                  ALU.mult).then_inc(s_pv, 1)

            def turn(s, r, g):
                static = isinstance(s, int)
                extract = not static or s < NB
                attend = not static or 4 <= s < NB + 4
                steps = block_steps(s - 4, r) if attend else ()
                for i in range(SCORE_STEPS):
                    if attend:
                        steps[i]()
                    if extract and i < NSEG:
                        search(s, i)
                if extract:
                    drop_self(s, r % 2)
                if attend:
                    denominators(s - 4, S1)
                if extract:
                    best(s, r % 2)
                if attend:
                    weigh_values(s - 4, r, S1)
                if static and g < 2:
                    return
                k = LN_B + g - 2
                if r == 1:
                    dve.wait_ge(s_x2, G * g - 4)
                    moments(k, group_rows(g - 2))
                if r == 2:
                    scale_rows(k)
                if r == 3:
                    normalise(k, group_rows(g - 2))

            for g in range(3):
                for r in range(G):
                    turn(G * g + r, r, g)
            with dve.Fori(3, NG) as g:
                for r in range(G):
                    turn(G * g + r, r, g)
            turn(NB, 0, NG)

            flagged = [1]

            def link(instruction):
                flagged[0] += 1
                instruction.then_inc(s_flag, 1)
                dve.wait_ge(s_flag, flagged[0])

            dve.wait_ge(s_gap, 3 * NB)
            link(dve.tensor_scalar(work[:, :, :], found[:, :, :], float(HALF), None, ALU.is_ge))
            link(dve.tensor_reduce(full[:, :, :], work[:, :, :].rearrange("p b (s k) -> p b s k", k=8), axis=AX_X,
                                   op=ALU.add))
            link(dve.tensor_reduce(count[:, :], full[:, :, :], axis=AX_X, op=ALU.add))
            link(dve.tensor_scalar(flag[:, :], count[:, :], 8.5, None, ALU.is_gt))
            link(dve.tensor_reduce(worst[:, :], full[:, :, :], axis=AX_X, op=ALU.max))
            link(dve.scalar_tensor_tensor(out=flag[:, :], in0=worst[:, :], scalar=6.5, in1=flag[:, :],
                                          op0=ALU.is_ge, op1=ALU.max))
            link(dve.tensor_reduce(worst[:, :], found[:, :, :], axis=AX_X, op=ALU.max))
            link(dve.scalar_tensor_tensor(out=flag[:, :], in0=worst[:, :], scalar=float(3 * HALF), in1=flag[:, :],
                                          op0=ALU.is_ge, op1=ALU.max))
            turn(NB + 1, 1, NG)

            dve.wait_ge(s_flag_ps, 1)
            link(dve.tensor_copy(totals[:, :], ps[:, ROWS, NB:2 * NB]))
            link(dve.tensor_tensor_scan(worst[:, :], totals[:, :], totals[:, :], 0.0, ALU.add, ALU.bypass))
            link(dve.tensor_tensor(place[:, :], worst[:, :], totals[:, :], ALU.subtract))
            link(dve.tensor_tensor(place[:, :], place[:, :], ps[:, ROWS, 0:NB], ALU.add))
            link(dve.scalar_tensor_tensor(out=place[:, :], in0=place[:, :], scalar=1.0, in1=flag[:, :],
                                          op0=ALU.add, op1=ALU.mult))
            assert flagged[0] == FLAG_STEPS, flagged[0]
            with dve.Fori(0, NB // G) as i:
                for r in range(G):
                    b = G * i + r
                    dve.wait_ge(s_pick_ps, b + 1)
                    dve.tensor_scalar(pick[:, r, :], rank[:, :], place[:, bass.ds(b, 1)], None,
                                      ALU.is_equal).then_inc(s_pick, 1)
            dve.wait_ge(s_pick_ps, NB + G)
            vn = [0]

            def vlink(instruction):
                vn[0] += 1
                instruction.then_inc(s_vnum, 1)
                dve.wait_ge(s_vnum, vn[0])

            vlink(dve.tensor_copy(vnum[:, 0:1], ps[:, UP, 0:1]))
            vlink(dve.tensor_scalar(vnum[:, 1:2], vnum[:, 0:1], 0.0, float(NO_ROW), ALU.is_equal, ALU.mult))
            vlink(dve.tensor_scalar(vnum[:, 2:3], vnum[:, 0:1], -1.0, COL2 + 1.0, ALU.mult, ALU.add))
            dve.scalar_tensor_tensor(out=vrow[:, :], in0=vnum[:, 0:1], scalar=-1.0, in1=vnum[:, 1:2],
                                     op0=ALU.add, op1=ALU.add).then_inc(s_vrow, 1)
            turn(NB + 2, 2, NG)

            for s in range(VSEG):
                dve.wait_ge(s_keys, ALL_KEYS + s + 1)
                dve.max(out=vcand[:, 8 * s:8 * s + 8], in_=ps[:, KEYS + s % RING, :]).then_inc(s_cand, 1)
            dve.wait_ge(s_cand, ALL_KEYS + VSEG)
            vs = [0]

            def slink(instruction):
                vs[0] += 1
                instruction.then_inc(s_vsearch, 1)
                dve.wait_ge(s_vsearch, vs[0])

            slink(dve.scalar_tensor_tensor(out=vclean[:, :], in0=vcand[:, :], scalar=vnum[:, 2:3], in1=vcand[:, :],
                                           op0=ALU.not_equal, op1=ALU.mult))
            slink(dve.max(out=vtop[:, 0:8], in_=vclean[:, :]))
            slink(dve.match_replace(out=vrest[:, :], in_to_replace=vtop[:, 0:8], in_values=vclean[:, :],
                                    imm_value=-1.0))
            dve.max(out=vtop[:, 8:16], in_=vrest[:, :]).then_inc(s_top, 1)
            slink(dve.tensor_scalar(vwork[:, :], vcand[:, :], vnum[:, 2:3], None, ALU.is_equal))
            slink(dve.tensor_reduce(vstat[:, 0:1], vwork[:, :], axis=AX_X, op=ALU.add))
            slink(dve.tensor_scalar(vgap[:, 0:1], vstat[:, 0:1], -1.0, 1.0, ALU.mult, ALU.add))
            slink(dve.tensor_scalar(vwork[:, :], vclean[:, :], float(N), None, ALU.is_ge))
            slink(dve.tensor_reduce(vstat[:, 1:2], vwork[:, :], axis=AX_X, op=ALU.add))
            slink(dve.tensor_reduce(vstat[:, 2:3], vcand[:, 7::8], axis=AX_X, op=ALU.max))
            slink(dve.tensor_reduce(vstat[:, 3:4], vcand[:, :], axis=AX_X, op=ALU.max))
            slink(dve.tensor_scalar(vstat[:, 4:5], vstat[:, 1:2], 16.5, None, ALU.is_gt))
            slink(dve.scalar_tensor_tensor(out=vstat[:, 4:5], in0=vstat[:, 2:3], scalar=float(N), in1=vstat[:, 4:5],
                                           op0=ALU.is_ge, op1=ALU.max))
            slink(dve.scalar_tensor_tensor(out=vstat[:, 4:5], in0=vstat[:, 3:4], scalar=float(2 * N),
                                           in1=vstat[:, 4:5], op0=ALU.is_ge, op1=ALU.max))
            slink(dve.scalar_tensor_tensor(out=vstat[:, 4:5], in0=vnum[:, 0:1], scalar=0.0, in1=vstat[:, 4:5],
                                           op0=ALU.is_gt, op1=ALU.mult))
            dve.scalar_tensor_tensor(out=vstat[:, 5:6], in0=worst[:, NB - 1:NB], scalar=P + 0.5, in1=vstat[:, 4:5],
                                     op0=ALU.is_gt, op1=ALU.max).then_inc(s_vcheck, 1)
            turn(NB + 3, 3, NG)
            dve.wait_ge(s_vcheck_ps, 1)
            dve.tensor_scalar(dense_flag[:, :], ps[:, X2, P:P + 1], -1.0 if force_dense else 0.5, None,
                              ALU.is_gt).then_inc(s_dense, 1)

            k = LN_B + NG - 1
            dve.wait_ge(s_x2, NB)
            moments(k, group_rows(NG - 1))
            scale_rows(k)
            normalise(k, group_rows(NG - 1))

            dve.wait_ge(s_vload, 48)
            dve.wait_ge(s_vgather, 256)
            dve.wait_ge(s_gap, 3 * NB + 1)
            for each in score_steps(NB, 0, vq[:, :, :], vgap[:, :]):
                each()
            denominators(NB, S2)
            weigh_values(NB, 0, S2)
            dve.wait_ge(s_x2, NB + 1)
            moments(LN_V, group_rows(NG), 1)
            scale_rows(LN_V)
            normalise(LN_V, group_rows(NG), 1)

            with where_dense(dve):
                dve.memset(smax[:, 0:1], 0.0).then_inc(d_adj_free, 1)
                with dve.Fori(0, NB) as b:
                    dve.wait_ge(d_adj, 16 * b + 16)
                    dve.tensor_scalar(bias, adj_sb[:, 0, :], 0.0, NEG, ALU.is_equal, ALU.mult).then_inc(d_bias, 1)
                    dve.wait_ge(d_bias, b + 1)
                    dve.memset(smax[:, 0:1], 0.0).then_inc(d_adj_free, 1)
                    dve.wait_ge(d_qT, b + 1)
                    dve.nop(nofuse=True)
                    with dve.Fori(0, H) as h:
                        t = H * b + h + 1
                        dve.tensor_scalar(xnT[:, 1, 0:P], xnT[:, 0, 0:P], head_cols[:, bass.ds(h, 1)], None,
                                          ALU.mult).then_inc(d_qh, 1)
                        dve.wait_ge(d_s_ps, t)
                        dve.tensor_tensor(s_all, ps[:, :, :].rearrange("p a m -> p (a m)"), bias,
                                          ALU.add).then_inc(d_s, 1)
                        dve.wait_ge(d_s, t)
                        dve.tensor_reduce(smax[:, 0:1], s_all, axis=AX_X, op=ALU.max).then_inc(d_max, 1)
                        dve.wait_ge(d_max, t)
                        dve.tensor_scalar(smax[:, 1:2], smax[:, 0:1], -SCALE, None, ALU.mult).then_inc(d_neg, 1)
                        dve.wait_ge(d_exp, t)
                        dve.reciprocal(rden[:, 0:1], den[:, 0:1]).then_inc(d_rden, 1)
                        for c in range(TURNS):
                            dve.wait_ge(d_pT_ps, TURNS * (t - 1) + c + 1)
                            dve.tensor_copy(pT[:, c % 2, :], ps[:, c % 2, :]).then_inc(d_pT, 1)
                        dve.wait_ge(d_o_ps, t)
                        dve.wait_ge(d_rden, t)
                        dve.tensor_scalar(att[:, bass.ts(h, DH)], ps[:, 7, 0:DH], rden[:, 0:1], None,
                                          ALU.mult).then_inc(d_o, 1)
                dve.wait_ge(d_x2, NB)
                with dve.Fori(0, NG) as g:
                    moments(LN_D + g, group_rows(g))
                    scale_rows(LN_D + g)
                    normalise(LN_D + g, group_rows(g))

        @block.tensor
        def _(pe):
            def transpose_rows(k, bank, j=0, width=G):
                pe.wait_ge(s_xn, k + 1)
                for i in range(width):
                    last = pe.transpose(ps[:, bank, i * P:(i + 1) * P], xn[:, j, i, :], ident[:, :])
                last.then_inc(s_xnT_ps, 1)

            pe.wait_ge(s_const, IDENT_MADE)
            pe.wait_ge(s_weights, 16 * NWEIGHTS)
            for k in range(1, NG + 3):
                if k <= NG:
                    wait_past(pe, s_xnT, k - 2)
                    transpose_rows(k - 1, 4 * ((k - 1) % 2), (k - 1) % 2)
                if 2 <= k < NG + 2:
                    c, j = k - 2, (k - 2) % 2
                    pe.wait_ge(s_xnT, c + 1)
                    wait_past(pe, s_q, c - 1)
                    for i in range(G):
                        last = pe.matmul(ps[:, 4 * j + 1, i * D:(i + 1) * D], xnT[:, j, i * P:(i + 1) * P],
                                         wqkv_sb[:, 0:D], start=True, stop=True)
                    last.then_inc(s_q_ps, 1)
                    wait_past(pe, s_kv, c - 1)
                    for i in range(G):
                        last = pe.matmul(ps[:, 4 * j + 2 + i // 2, 2 * D * (i % 2):2 * D * (i % 2 + 1)],
                                         xnT[:, j, i * P:(i + 1) * P], wqkv_sb[:, D:3 * D], start=True, stop=True)
                    last.then_inc(s_kv_ps, 1)
            pe.wait_ge(s_q, NG)
            pe.wait_ge(s_kv, NG)
            pe.wait_ge(s_const, NCONST)

            def keys(b, j):
                pe.wait_ge(s_mask, b + 1)
                for s in range(NSEG):
                    wait_past(pe, s_cand, NSEG * (b - 1) + s + 1)
                    low, high = slice(SEG * s, SEG * (s + 1)), slice(HALF + SEG * s, HALF + SEG * (s + 1))
                    bank = ps[:, KEYS + s, :]
                    pe.matmul(bank, ident_2[:, :], mask[:, j, low], start=True, stop=False)
                    pe.matmul(bank, ident_1[:, :], mask[:, j, high], start=False, stop=False)
                    pe.matmul(bank, ones33[:, :], column_key[:, high], start=False, stop=True).then_inc(s_keys, 1)

            def attention_out(b, j, n=S1):
                wait_past(pe, s_oT, b)
                pe.wait_ge(s_pv, b + 1)
                for s in range(n):
                    last = pe.matmul(ps[:, OUT_T, 0:P], pv[j][:, s, :], ident[:, :], start=(s == 0), stop=(s == n - 1))
                last.then_inc(s_oT_ps, 1)
                wait_past(pe, s_x2, b)
                pe.matmul(ps[:, X2, 0:D], ident[:, :], block_of(xs, b), start=True, stop=False)
                pe.matmul(ps[:, X2, 0:D], ones[0:1, :], bproj_row[:, :], start=False, stop=False)
                pe.wait_ge(s_oT, b + 1)
                pe.matmul(ps[:, X2, 0:D], oT[:, j, :], wproj_sb[:, :], start=False, stop=True).then_inc(s_x2_ps, 1)

            def up(kf, k, width=G):
                pe.wait_ge(s_xnT, k + 1)
                wait_past(pe, s_res, kf)
                for c in range(FC):
                    wait_past(pe, s_g, FC * kf + c - 1)
                    pe.matmul(ps[:, (UP, ROWS)[c % 2], 0:width * P], w1_sb[:, c * P:(c + 1) * P],
                              xnT[:, 0, 0:width * P], start=True, stop=True).then_inc(s_u_ps, 1)

            def down(kf, g, width=G):
                pe.wait_ge(s_g, FC * kf + FC)
                for i in range(width):
                    bank = ps[:, UP, i * D:(i + 1) * D]
                    for c in range(FC):
                        pe.matmul(bank, gT[:, c, i * P:(i + 1) * P], w2_sb[:, c, :], start=(c == 0), stop=False)
                    pe.matmul(bank, ones[0:1, :], b2_row[:, :], start=False, stop=False)
                    last = pe.matmul(bank, ident[:, :], block_of(xs, G * g + i), start=False, stop=True)
                last.then_inc(s_ff, 1)

            def turn(s, r, g):
                static = isinstance(s, int)
                if not static or s < NB:
                    keys(s, r % 2)
                if not static or 5 <= s < NB + 5:
                    attention_out(s - 5, (r + 1) % 2)
                if r == 2 and (not static or g >= 3):
                    up(g - 3, LN_B + g - 3)
                if r == 3 and (not static or g >= 3):
                    down(g - 3, g - 3)
                if r == 3 and (not static or g >= 2):
                    transpose_rows(LN_B + g - 2, ROWS)

            for g in range(4):
                for r in range(G):
                    turn(G * g + r, r, g)
            with pe.Fori(4, NG) as g:
                for r in range(G):
                    turn(G * g + r, r, g)
            turn(NB, 0, NG)
            pe.wait_ge(s_flag, 9)
            pe.wait_ge(s_xnT, LN_B + NG - 2)
            pe.matmul(ps[:, ROWS, 0:NB], before[:, :], flag[:, :], start=True, stop=True)
            pe.matmul(ps[:, ROWS, NB:2 * NB], ones[:, :], flag[:, :], start=True, stop=True).then_inc(s_flag_ps, 1)
            turn(NB + 1, 1, NG)
            pe.wait_ge(s_flag, FLAG_STEPS)
            pe.wait_ge(s_res, NG - 3)
            pe.matmul(ps[:, UP, 0:1], ident[:, :], before[:, 0:1], start=True, stop=True).then_inc(s_pick_ps, G)
            with pe.Fori(0, NB // G) as i:
                for r in range(G):
                    b = G * i + r
                    pe.wait_ge(s_pick, b + 1)
                    pe.matmul(ps[:, UP, 0:1], pick[:, r, :], row_number[:, bass.ds(b, 1)], start=False,
                              stop=True, skip_group_check=True).then_inc(s_pick_ps, 1)
            pe.wait_ge(s_vnum, 1)
            turn(NB + 2, 2, NG)
            pe.wait_ge(s_mask, NB + 1)
            for s in range(VSEG):
                pe.wait_ge(s_cand, ALL_KEYS + s - RING + 1)
                cols = slice(SEG * s, SEG * (s + 1))
                pe.matmul(ps[:, KEYS + s % RING, :], ident_2[:, :], mask[:, 0, cols], start=True, stop=False)
                pe.matmul(ps[:, KEYS + s % RING, :], ones33[:, :], column_key[:, cols], start=False,
                          stop=True).then_inc(s_keys, 1)
            turn(NB + 3, 3, NG)
            pe.wait_ge(s_vcheck, 1)
            pe.wait_ge(s_x2, NB - 1)
            pe.matmul(ps[:, X2, P:P + 1], ones[:, :], vstat[:, 5:6], start=True, stop=True).then_inc(s_vcheck_ps, 1)
            pe.wait_ge(s_dense, 1)
            attention_out(NB - 1, 1)
            up(NG - 2, LN_B + NG - 2)
            down(NG - 2, NG - 2)
            transpose_rows(LN_B + NG - 1, ROWS)
            up(NG - 1, LN_B + NG - 1)
            down(NG - 1, NG - 1)
            attention_out(NB, 0, S2)
            transpose_rows(LN_V, ROWS, width=1)
            up(FF_V, LN_V, 1)
            down(FF_V, NG, 1)

            with where_dense(pe):
                with pe.Fori(0, NB) as c:
                    pe.wait_ge(d_copied, c + 1)
                    pe.transpose(ps[:, 0, 0:P], xn[:, 0, 0, :], ident[:, :]).then_inc(d_kT_ps, 1)
                pe.wait_ge(d_kT, NB)
                pe.wait_ge(d_x, 16)
                with pe.Fori(0, NB) as b:
                    pe.wait_ge(d_q, b + 1)
                    pe.transpose(ps[:, 1, 0:P], xn[:, 1, 0, :], ident[:, :]).then_inc(d_qT_ps, 1)
                    with pe.Fori(0, H) as h:
                        t = H * b + h + 1
                        pe.wait_ge(d_qh, t)
                        for c in range(TURNS):
                            last = pe.matmul(ps[:, c, :], xnT[:, 1, 0:P], kT[:, bass.ts(c, 512)], start=True, stop=True)
                        last.then_inc(d_s_ps, 1)
                        pe.wait_ge(d_exp, t)
                        for c in range(TURNS + 1):
                            if c < TURNS:
                                if c >= 2:
                                    pe.wait_ge(d_pT, TURNS * (t - 1) + c - 1)
                                for r in range(4):
                                    last = pe.transpose(ps[:, c % 2, bass.ts(r, P)],
                                                        s_all[:, bass.ts(4 * c + r, P)], ident[:, :])
                                last.then_inc(d_pT_ps, 1)
                            if c >= 1:
                                pe.wait_ge(d_pT, TURNS * (t - 1) + c)
                                for r in range(4):
                                    m = 4 * (c - 1) + r
                                    last = pe.matmul(ps[:, 7, 0:DH], pT[:, (c - 1) % 2, bass.ts(r, P)],
                                                     v_all[:, m, bass.ts(h, DH)], start=(m == 0), stop=(m == NB - 1))
                        last.then_inc(d_o_ps, 1)
                    pe.wait_ge(d_o, H * b + H)
                    pe.transpose(ps[:, 0, 0:P], att, ident[:, :]).then_inc(d_oT_ps, 1)
                    pe.matmul(ps[:, 2, 0:D], ident[:, :], block_of(xs, b), start=True, stop=False)
                    pe.matmul(ps[:, 2, 0:D], ones[0:1, :], bproj_row[:, :], start=False, stop=False)
                    pe.wait_ge(d_oT, b + 1)
                    pe.matmul(ps[:, 2, 0:D], oT[:, 0, :], wproj_sb[:, :], start=False, stop=True).then_inc(d_x2_ps, 1)
                pe.wait_ge(d_x2, NB)
                with pe.Fori(0, NG) as g:
                    transpose_rows(LN_D + g, ROWS)
                    up(FF_D + g, LN_D + g)
                    down(FF_D + g, g)


_INS = ["x", "adj", "L0_gnn_w_qkv", "L0_gnn_w_proj", "L0_gnn_b_proj", "L0_gnn_w1", "L0_gnn_b1", "L0_gnn_w2",
        "L0_gnn_b2", "L0_gnn_g1", "L0_gnn_be1", "L0_gnn_g2", "L0_gnn_be2"]


def kernel(**inputs):
    import numpy as _np
    import concourse.bacc as _bacc
    from concourse import mybir as _mybir
    from concourse.bass_utils import run_bass_kernel_spmd as _run

    nc = _bacc.Bacc("TRN2", target_bir_lowering=False, num_devices=1)
    arrays, args = {}, []
    for name in _INS:
        a = _np.ascontiguousarray(inputs[name])
        arrays[f"in_{name}"] = a
        args.append(nc.dram_tensor(f"in_{name}", a.shape, _mybir.dt.from_np(a.dtype), kind="ExternalInput").ap())
    out = nc.dram_tensor("out_rows", (N, D), F32, kind="ExternalOutput").ap()
    graph_layer(nc, *args, out)
    r = _run(nc, [arrays], core_ids=[0])
    return r.results[0]["out_rows"]
```

```python
from contextlib import ExitStack

import concourse.bass as bass
from concourse import mybir


F32 = mybir.dt.float32
BF16 = mybir.dt.bfloat16
I32 = mybir.dt.int32
U32 = mybir.dt.uint32
ALU = mybir.AluOpType
ACT = mybir.ActivationFunctionType
AX_X = mybir.AxisListType.X

P = 128
N = 4096
D = 128
H = 8
DH = D // H
FF = 512
FC = FF // P
NB = N // P
SCALE = float(DH) ** -0.5
EPS = 1e-5
NEG = -1.0e30

SEG = 512
RING = 3
G = 4
NG = NB // G
RINGS = 4
LEAD = 2 * G
HALF = N // 2
NSEG = HALF // SEG
VSEG = N // SEG
SELF = 1
S1 = SELF + 8
S2 = SELF + 16
COL1 = float(HALF + N - 1)
COL2 = float(2 * N - 1)
NO_ROW = 2 * N


def block_of(tile, b):
    return tile[:, bass.ds(b, 1), :].rearrange("p a d -> p (a d)")


def wait_past(eng, sem, count):
    if not isinstance(count, int) or count > 0:
        eng.wait_ge(sem, count)


def over_heads(tile, slots):
    return tile.rearrange("p (s a) -> p s a", a=1).to_broadcast([P, slots, H])


def over_slots(tile, slots):
    return tile.rearrange("p (a h) -> p a h", a=1).to_broadcast([P, slots, H])


def graph_layer(nc, x, adj, w_qkv, w_proj, b_proj, w1, b1, w2, b2, g1, be1, g2, be2, out, force_dense=False):
    kv_dram = nc.dram_tensor("kv_table", [N, 2 * D], F32).ap()
    q_dram = nc.dram_tensor("q_table", [N, D], F32).ap()
    x_cols = x.rearrange("(b p) d -> p b d", p=P)
    out_rows = out.rearrange("(b p) d -> b p d", p=P)
    adj_rows = adj.rearrange("(b p) m -> b p m", p=P)
    kv_rows = kv_dram.rearrange("(b p) d -> b p d", p=P)

    ctx = ExitStack()
    with ctx:
        def sb(name, shape, dt=F32):
            return ctx.enter_context(nc.sbuf_tensor(name, shape, dt))

        def sem(name):
            return ctx.enter_context(nc.semaphore(name))

        ident = sb("ident", [P, P])
        ident_1 = sb("ident_1", [P, P], BF16)
        ident_2 = sb("ident_2", [P, P], BF16)
        ones33 = sb("ones33", [33, P], BF16)
        column_key = sb("column_key", [33, N], BF16)
        ones = sb("ones", [P, P])
        before = sb("before", [P, P])
        rank = sb("rank", [P, P])
        row_number = sb("row_number", [P, NB, 2], BF16)
        self_key = sb("self_key", [P, NB])
        head_cols = sb("head_cols", [P, H])
        consts = sb("consts", [P, 4])
        col1, half_col, col2, n_col = (consts[:, i:i + 1] for i in range(4))
        wqkv_sb = sb("wqkv_sb", [P, 3 * D])
        wproj_sb = sb("wproj_sb", [P, D])
        w1_sb = sb("w1_sb", [P, FF])
        w2_sb = sb("w2_sb", [P, FC, D])
        bproj_row = sb("bproj_row", [1, D])
        b2_row = sb("b2_row", [1, D])
        b1_col = sb("b1_col", [P, FC])
        ln_cols = sb("ln_cols", [P, 4])
        diag = sb("diag", [P, NB], I32)

        xs = sb("xs", [P, NB + 1, D])
        qs = sb("qs", [P, NB, D])
        slots = sb("slots", [P, RINGS * S1 + S2, 2 * D])
        vq = sb("vq", [P, 1, D])
        adj_sb = sb("adj_sb", [P, 2, N], I32)
        mask = sb("mask", [P, 2, N], BF16)

        stats = sb("stats", [P, 2, G, 6])
        mean = sb("mean", [P, 2, G])
        var = sb("var", [P, 2, G])
        half = sb("half", [P, 2, G])
        rstd = sb("rstd", [P, 2, G])
        shift = sb("shift", [P, 2, G])
        xn = sb("xn", [P, 2, G, D])
        xnT = sb("xnT", [P, 2, G * P])

        cand = sb("cand", [P, NSEG * 8])
        clean = sb("clean", [P, 2, NSEG * 8])
        found = sb("found", [P, NB, NSEG * 8])
        top = sb("top", [P, 2, 8])
        gap = sb("gap", [P, NB, S1])
        best_keys = sb("best_keys", [P, NB, 8])
        idx = sb("idx", [P, RINGS, 8], I32)
        vcand = sb("vcand", [P, VSEG * 8])
        vclean = sb("vclean", [P, VSEG * 8])
        vrest = sb("vrest", [P, VSEG * 8])
        vtop = sb("vtop", [P, 16])
        vgap = sb("vgap", [P, S2])
        vidx = sb("vidx", [P, 16], I32)
        flag = sb("flag", [P, NB])
        full = sb("full", [P, NB, NSEG])
        count = sb("count", [P, NB])
        worst = sb("worst", [P, NB])
        totals = sb("totals", [P, NB])
        place = sb("place", [P, NB])
        vnum = sb("vnum", [P, 4])
        vrow = sb("vrow", [P, 1], I32)
        vwork = sb("vwork", [P, VSEG * 8])
        vstat = sb("vstat", [P, 6])
        dense_flag = sb("dense_flag", [P, 1], I32)

        prod = sb("prod", [P, S2, D])
        sc = sb("sc", [P, S2, H])
        smax = sb("smax", [P, H])
        ex = sb("ex", [P, S2, H])
        den = sb("den", [P, H])
        rden = sb("rden", [P, H])
        pr = sb("pr", [P, S2, H])
        pv0 = sb("pv0", [P, S2, D])
        pv1 = sb("pv1", [P, S1, D])
        pv = (pv0, pv1)
        work = prod[:, S1:S2, :].rearrange("p s (b k) -> p (s b) k", k=NSEG * 8)
        pick = mask[:, 1, :].rearrange("p (b n) -> p b n", n=P)
        PICKS = 4
        oT = sb("oT", [P, 2, P])
        gT = sb("gT", [P, FC, G * P])
        res = sb("res", [P, G, D])
        ps = ctx.enter_context(nc.psum_tensor("ps", [P, 8, 512], F32))
        A_ROWS, A_Q, A_KV, A_KEYS = 0, 1, 2, 4
        ATT, ROWS, UP, RES, UP2, KEYS = 0, 1, 2, 3, 4, 5
        UP_BANKS = (UP, RES, ROWS, UP2)
        KEY_BANKS = [KEYS + i % RING for i in range(NSEG)]
        SUMS, LIST, CHECK = KEYS, KEYS + 1, KEYS

        s_const = sem("s_const")
        s_key_rows = sem("s_key_rows")
        s_wqkv = sem("s_wqkv")
        s_weights = sem("s_weights")
        s_diag = sem("s_diag")
        s_x = [sem(f"s_x_part{i}") for i in range(4)]
        s_adj = [sem("s_adj0"), sem("s_adj1")]
        s_moments = sem("s_moments")
        s_sqrt = sem("s_sqrt")
        s_rstd = sem("s_rstd")
        s_shift = sem("s_shift")
        s_xn = sem("s_xn")
        s_xnT_ps = sem("s_xnT_ps")
        s_xnT = sem("s_xnT")
        s_q_ps = sem("s_q_ps")
        s_kv_ps = sem("s_kv_ps")
        s_q = sem("s_q")
        s_kv = sem("s_kv")
        s_kv_stored = sem("s_kv_stored")
        s_q_stored = sem("s_q_stored")
        s_self = [sem(f"s_self{i}") for i in range(RINGS)]
        s_mask = sem("s_mask")
        s_keys = sem("s_keys")
        s_cand = sem("s_cand")
        s_clean = sem("s_clean")
        s_top = sem("s_top")
        s_idx = sem("s_idx")
        s_gap = sem("s_gap")
        s_gather = [sem(f"s_gather{i}") for i in range(RINGS)]
        s_flag = sem("s_flag")
        s_flag_ps = sem("s_flag_ps")
        s_pick = sem("s_pick")
        s_pick_ps = sem("s_pick_ps")
        s_vnum = sem("s_vnum")
        s_vrow = sem("s_vrow")
        s_vadj = sem("s_vadj")
        s_vload = sem("s_vload")
        s_vsearch = sem("s_vsearch")
        s_vcheck = sem("s_vcheck")
        s_vcheck_ps = sem("s_vcheck_ps")
        s_vgather = sem("s_vgather")
        s_dense = sem("s_dense")
        s_score = sem("s_score")
        s_exp = sem("s_exp")
        s_soft = sem("s_soft")
        s_pv = sem("s_pv")
        s_oT_ps = sem("s_oT_ps")
        s_oT = sem("s_oT")
        s_x2_ps = sem("s_x2_ps")
        s_x2 = sem("s_x2")
        s_u_ps = sem("s_u_ps")
        s_g = sem("s_g")
        s_ff = sem("s_ff")
        s_res = sem("s_res")
        s_out = sem("s_out")
        s_vout = sem("s_vout")

        d_load = sem("d_load")
        d_copied = sem("d_copied")
        d_kT_ps = sem("d_kT_ps")
        d_kT = sem("d_kT")
        d_x = sem("d_x")
        d_adj_free = sem("d_adj_free")
        d_adj = sem("d_adj")
        d_bias = sem("d_bias")
        d_q = sem("d_q")
        d_qT_ps = sem("d_qT_ps")
        d_qT = sem("d_qT")
        d_qh = sem("d_qh")
        d_s_ps = sem("d_s_ps")
        d_s = sem("d_s")
        d_max = sem("d_max")
        d_neg = sem("d_neg")
        d_exp = sem("d_exp")
        d_rden = sem("d_rden")
        d_pT_ps = sem("d_pT_ps")
        d_pT = sem("d_pT")
        d_o_ps = sem("d_o_ps")
        d_o = sem("d_o")
        d_oT_ps = sem("d_oT_ps")
        d_oT = sem("d_oT")
        d_x2_ps = sem("d_x2_ps")
        d_x2 = sem("d_x2")

        kT = slots[:, 0:16, :].rearrange("p s d -> p (s d)")
        v_all = slots[:, 16:32, :].rearrange("p s (a d) -> p (s a) d", a=2)
        bias = adj_sb[:, 1, :].bitcast(F32)
        s_all = mask[:, :, :].rearrange("p a m -> p (a m)").bitcast(F32)
        pT = gT[:, 0:2, :]
        att = prod[:, 0, :]
        TURNS = 8

        block = ctx.enter_context(nc.Block())

        def where_dense(eng):
            eng.wait_ge(s_dense, 1)
            eng.wait_ge(s_res, NG + 1)
            return eng.If(eng.value_load(dense_flag[0:1, 0:1], min_val=0, max_val=1) > 0)

        NWQKV, NWEIGHTS = 3, 8
        NCONST = 26
        IDENT_MADE, KEYS_MADE = 2, 14
        SCORE_STEPS = 5
        FLAG_STEPS = 14
        ALL_KEYS = NSEG * NB
        LN_B, LN_V, LN_D = NG, 2 * NG, 2 * NG + 1
        FF_V, FF_D = NG, NG + 1

        def slot_tile(b, r):
            if isinstance(b, int) and b == NB:
                return slots[:, RINGS * S1:RINGS * S1 + S2, :], S2
            return slots[:, S1 * r:S1 * (r + 1), :], S1

        def ring_count(b, r, per):
            if isinstance(b, int):
                return per * (b // RINGS + 1)
            return (per // RINGS) * (b - r) + per

        def blocks_of(tile, g, width=None):
            if width is not None and width != G:
                return tile[:, NB:NB + width, :]
            return tile[:, bass.ts(g, G), :]

        @block.sync
        def _(sp):
            for c in range(4):
                w = NB // 4
                sp.dma_start(xs[:, w * c:w * (c + 1), :], x_cols[:, w * c:w * (c + 1), :]).then_inc(s_x[c], 16)

            def load_adj(b, j):
                wait_past(sp, s_mask, b - 1)
                sp.dma_start(adj_sb[:, j, :], adj_rows[b, :, :]).then_inc(s_adj[j], 16)

            def load_self(b, r):
                wait_past(sp, s_pv, b - RINGS + 1)
                sp.dma_start(slots[:, S1 * r, :], kv_rows[b, :, :]).then_inc(s_self[r], 16)

            def store(g):
                sp.wait_ge(s_res, g + 1)
                sp.dma_start(out_rows[bass.ts(g, G), :, :].rearrange("b p d -> p b d"),
                             res[:, :, :]).then_inc(s_out, 16)

            sp.wait_ge(s_wqkv, 16 * NWQKV)
            for b in range(LEAD + 2):
                if b >= 5 and b % 2 == 1:
                    c, w = (b - 5) // 2, 2 * G
                    sp.wait_ge(s_kv, 2 * c + 2)
                    sp.dma_start(kv_rows[w * c:w * (c + 1), :, :].rearrange("b p d -> p b d"),
                                 slots[:, w * c:w * (c + 1), :]).then_inc(s_kv_stored, 16)
                load_adj(b, b % 2)
            c = NG // 2 - 1
            sp.wait_ge(s_kv, NG)
            sp.dma_start(kv_rows[w * c:w * (c + 1), :, :].rearrange("b p d -> p b d"),
                         slots[:, w * c:w * (c + 1), :]).then_inc(s_kv_stored, 16)
            sp.wait_ge(s_kv_stored, 16 * (NG // 2))
            for b in range(2):
                load_self(b, b)

            def turn(a, r):
                if not isinstance(a, int) or a + LEAD + 2 < NB:
                    load_adj(a + LEAD + 2, r % 2)
                if not isinstance(a, int) or a + 2 < NB:
                    load_self(a + 2, (r + 2) % RINGS)

            for g in range(3):
                for r in range(G):
                    turn(G * g + r, r)
            with sp.Fori(3, NG - 3) as g:
                for r in range(G):
                    turn(G * g + r, r)
                    if r == 2:
                        store(g - 3)
            for g in range(NG - 3, NG):
                for r in range(G):
                    turn(G * g + r, r)
                    if r == 2:
                        store(g - 3)
                if g == NG - 3:
                    sp.wait_ge(s_q, NG)
                    sp.dma_start(q_dram.rearrange("(b p) d -> p b d", p=P), qs[:, :, :]).then_inc(s_q_stored, 16)
            for g in range(NG - 3, NG):
                store(g)
            sp.wait_ge(s_out, 16 * NG)

            with where_dense(sp):
                kv_cols = kv_dram.rearrange("(b p) d -> p b d", p=P)
                sp.wait_ge(s_vout, 16)
                sp.dma_start(xs[:, 0:NB, :], kv_cols[:, :, 0:D]).then_inc(d_load, 16)
                sp.dma_start(v_all, kv_cols[:, :, D:2 * D]).then_inc(d_load, 16)
                sp.wait_ge(d_copied, NB)
                sp.dma_start(xs[:, 0:NB, :], x_cols).then_inc(d_x, 16)
                with sp.Fori(0, NB) as b:
                    sp.wait_ge(d_adj_free, b + 1)
                    sp.dma_start(adj_sb[:, 0, :], adj_rows[b, :, :]).then_inc(d_adj, 16)
                with sp.Fori(0, NG) as g:
                    sp.wait_ge(s_res, FF_D + g + 1)
                    sp.dma_start(out_rows[bass.ts(g, G), :, :].rearrange("b p d -> p b d"),
                                 res[:, :, :]).then_inc(s_out, 16)
                sp.wait_ge(s_out, 32 * NG)

        @block.gpsimd
        def _(pool):
            made = [0]

            def step(instruction):
                made[0] += 1
                instruction.then_inc(s_const, 1)
                pool.wait_ge(s_const, made[0])

            step(pool.memset(ident[:, :], 0.0))
            step(pool.affine_select(out=ident[:, :], in_=ident[:, :], compare_op=ALU.not_equal, fill=1.0,
                                    base=0, pattern=[[-1, P]], channel_multiplier=1))
            assert made[0] == IDENT_MADE
            for tile, value in ((ident_1, float(HALF)), (ident_2, float(N))):
                step(pool.memset(tile[:, :], 0.0))
                step(pool.affine_select(out=tile[:, :], in_=tile[:, :], compare_op=ALU.not_equal, fill=value,
                                        base=0, pattern=[[-1, P]], channel_multiplier=1))
            step(pool.memset(ones33[:, :], 1.0))
            for col, value in ((col1, COL1), (half_col, float(HALF)), (col2, COL2), (n_col, float(N))):
                step(pool.memset(col, value))
            pool.wait_ge(s_key_rows, 1)

            def number_columns(cols):
                n = (cols.stop - cols.start) // 64
                step(pool.iota(column_key[0:1, cols], pattern=[[-64, n], [0, 64]], base=N - 64 - cols.start,
                               channel_multiplier=0, allow_small_or_imprecise_dtypes=True))
                step(pool.iota(column_key[32:33, cols], pattern=[[0, n], [-1, 64]], base=63, channel_multiplier=0,
                               allow_small_or_imprecise_dtypes=True))

            number_columns(slice(HALF, N))
            step(pool.iota(self_key[:, :], pattern=[[-P, NB]], base=int(COL1), channel_multiplier=-1,
                           allow_small_or_imprecise_dtypes=True))
            assert made[0] == KEYS_MADE, made[0]
            number_columns(slice(0, HALF))
            step(pool.memset(ones[:, :], 1.0))
            step(pool.memset(slots[:, NB:RINGS * S1 + S2, :], 0.0))
            step(pool.affine_select(out=before[:, :], in_=ones[:, :], compare_op=ALU.is_gt, fill=0.0,
                                    base=0, pattern=[[1, P]], channel_multiplier=-1))
            step(pool.iota(rank[:, :], pattern=[[1, P]], base=1, channel_multiplier=0,
                           allow_small_or_imprecise_dtypes=True))
            step(pool.iota(row_number[:, :, 0], pattern=[[P, NB]], base=0, channel_multiplier=0,
                           allow_small_or_imprecise_dtypes=True))
            step(pool.iota(row_number[:, :, 1], pattern=[[0, NB]], base=1, channel_multiplier=1,
                           allow_small_or_imprecise_dtypes=True))
            step(pool.affine_select(out=head_cols[:, :], in_=ones[:, 0:H], compare_op=ALU.is_ge, fill=0.0,
                                    base=0, pattern=[[-DH, H]], channel_multiplier=1))
            step(pool.affine_select(out=head_cols[:, :], in_=head_cols[:, :], compare_op=ALU.is_ge, fill=0.0,
                                    base=DH - 1, pattern=[[DH, H]], channel_multiplier=-1))
            step(pool.memset(xs[:, NB, :], 0.0))
            step(pool.memset(vq[:, 0, :], 0.0))
            assert made[0] == NCONST, made[0]

            def gather_rows(dst, table, row, sem):
                pool.indirect_dma_start(out=dst, out_offset=None, in_=table,
                                        in_offset=bass.IndirectOffsetOnAxis(ap=row.bitcast(U32), axis=0),
                                        bounds_check=N - 1, oob_is_err=False).then_inc(sem, 16)

            def gather(b, r):
                pool.wait_ge(s_idx, b + 1)
                wait_past(pool, s_pv, b - RINGS + 1)
                pool.nop(nofuse=True)
                for s in range(8):
                    gather_rows(slots[:, S1 * r + SELF + s, :], kv_dram[:, :], idx[:, r, s:s + 1], s_gather[r])

            pool.wait_ge(s_kv_stored, 16 * (NG // 2))
            for b in range(G):
                gather(b, b)
            with pool.Fori(1, NG - 1) as g:
                for r in range(G):
                    gather(G * g + r, r)

            for r in range(2):
                gather(NB - G + r, r)

            pool.wait_ge(s_vrow, 1)
            pool.wait_ge(s_mask, NB)
            gather_rows(adj_sb[:, 0, :], adj[:, :], vrow[:, 0:1], s_vadj)
            for r in range(2, G):
                gather(NB - G + r, r)
            pool.wait_ge(s_q_stored, 16)
            gather_rows(slots[:, RINGS * S1, :], kv_dram[:, :], vrow[:, 0:1], s_vload)
            gather_rows(vq[:, 0, :], q_dram[:, :], vrow[:, 0:1], s_vload)
            gather_rows(xs[:, NB, :], x[:, :], vrow[:, 0:1], s_vload)
            pool.wait_ge(s_idx, NB + 1)
            for s in range(16):
                gather_rows(slots[:, RINGS * S1 + SELF + s, :], kv_dram[:, :], vidx[:, s:s + 1], s_vgather)

            pool.wait_ge(s_out, 16 * NG)
            pool.wait_ge(s_res, NG + 1)
            pool.indirect_dma_start(out=out[:, :], out_offset=bass.IndirectOffsetOnAxis(
                ap=vrow[:, 0:1].bitcast(U32), axis=0), in_=res[:, 0, :], in_offset=None,
                bounds_check=N - 1, oob_is_err=False).then_inc(s_vout, 16)
            pool.wait_ge(s_vout, 16)

        @block.scalar
        def _(act):
            for dst, src in ((ln_cols[:, 0:1], g1.rearrange("(p a) -> p a", a=1)),
                             (ln_cols[:, 1:2], be1.rearrange("(p a) -> p a", a=1)),
                             (wqkv_sb[:, :], w_qkv)):
                act.dma_start(dst, src, allow_slow_non_contiguous=True).then_inc(s_wqkv, 16)
            for dst, src in ((wproj_sb[:, :], w_proj), (w1_sb[:, :], w1),
                             (w2_sb[:, :, :], w2.rearrange("(c p) n -> p c n", p=P)),
                             (bproj_row[:, :], b_proj.rearrange("(a n) -> a n", a=1)),
                             (b2_row[:, :], b2.rearrange("(a n) -> a n", a=1)),
                             (b1_col[:, :], b1.rearrange("(c p) -> p c", p=P)),
                             (ln_cols[:, 2:3], g2.rearrange("(p a) -> p a", a=1)),
                             (ln_cols[:, 3:4], be2.rearrange("(p a) -> p a", a=1))):
                act.dma_start(dst, src, allow_slow_non_contiguous=True).then_inc(s_weights, 16)
            act.dma_start(diag[:, :], bass.AP(tensor=adj.tensor, offset=0, ap=[[N + 1, P], [P * (N + 1), NB]]),
                          allow_slow_non_contiguous=True).then_inc(s_diag, 16)

            def deviation(k, j=0, before=1):
                act.wait_ge(s_moments, 7 * k + 7)
                wait_past(act, s_xn, k - before + 1)
                act.activation(rstd[:, j, :], var[:, j, :], ACT.Sqrt).then_inc(s_sqrt, 1)

            def keep_rows_T(k, bank, norm, j=0, width=G):
                act.wait_ge(s_xnT_ps, k + 1)
                w = width * P
                act.activation(xnT[:, j, 0:w], ps[:, bank, 0:w], ACT.Identity, scale=ln_cols[:, 2 * norm:2 * norm + 1],
                               bias=ln_cols[:, 2 * norm + 1:2 * norm + 2]).then_inc(s_xnT, 1)

            def make_mask(b, j):
                act.wait_ge(s_adj[j], 8 * (b - j) + 16)
                wait_past(act, s_keys, NSEG * (b - 1))
                act.activation(mask[:, j, :], adj_sb[:, j, :], ACT.Square).then_inc(s_mask, 1)

            def keep_keys(b, j):
                act.wait_ge(s_top, b + 1)
                act.activation(block_of(best_keys, b), top[:, j, :], ACT.Copy).then_inc(s_gap, 1)
                act.activation(gap[:, bass.ds(b, 1), SELF:S1].rearrange("p a s -> p (a s)"), top[:, j, :], ACT.Relu,
                               scale=-1.0, bias=half_col).then_inc(s_gap, 1)
                act.activation(block_of(found, b), clean[:, j, :], ACT.Copy).then_inc(s_gap, 1)

            def slot_numbers(b, r):
                wait_past(act, s_gap, 3 * (b + 1))
                wait_past(act, s_gather[r], ring_count(b, r, 128) - 128)
                act.activation(idx[:, r, :], block_of(best_keys, b), ACT.Relu, scale=-1.0, bias=col1).then_inc(s_idx, 1)

            act.wait_ge(s_wqkv, 16 * NWQKV)
            for k in range(NG + 3):
                if 2 <= k <= LEAD + 1:
                    make_mask(k - 1, (k - 1) % 2)
                if k >= 3:
                    act.wait_ge(s_q_ps, k - 2)
                    act.activation(qs[:, G * (k - 3):G * (k - 2), :].rearrange("p b d -> p (b d)"),
                                   ps[:, A_Q, :], ACT.Copy).then_inc(s_q, 1)
                if 1 <= k <= NG:
                    wait_past(act, s_kv_ps, k - 2)
                    keep_rows_T(k - 1, A_ROWS, 0, (k - 1) % 2)
                if k < NG:
                    deviation(k, k % 2, 2)
                if k == 1:
                    make_mask(0, 0)
                if k >= 3:
                    if k == 3:
                        act.wait_ge(s_const, KEYS_MADE)
                    keep_keys(k - 3, (k - 3) % 2)
            for b in range(RINGS):
                slot_numbers(b, b)
            act.wait_ge(s_weights, 16 * NWEIGHTS)

            def exponentials(b, n=S1):
                act.wait_ge(s_score, SCORE_STEPS * (b + 1))
                wait_past(act, s_soft, 3 * b)
                act.activation(ex[:, 0:n, :], sc[:, 0:n, :], ACT.Exp, scale=SCALE).then_inc(s_exp, 1)

            def keep_sum(b, j):
                act.wait_ge(s_oT_ps, b + 1)
                act.activation(oT[:, j, :], ps[:, ATT, 0:P], ACT.Copy).then_inc(s_oT, 1)

            def keep_x2(b):
                act.wait_ge(s_x2_ps, b + 1)
                act.activation(block_of(xs, b), ps[:, ATT, P:P + D], ACT.Copy).then_inc(s_x2, 1)

            def gelu_up(kf, width=G, chunks=range(FC)):
                w = width * P
                for c in chunks:
                    act.wait_ge(s_u_ps, FC * kf + c + 1)
                    wait_past(act, s_ff, kf)
                    act.activation(gT[:, c, 0:w], ps[:, UP_BANKS[c], 0:w], ACT.Gelu_apprx_tanh,
                                   bias=b1_col[:, c:c + 1]).then_inc(s_g, 1)

            def keep_result(kf, width=G, stored=None):
                act.wait_ge(s_ff, kf + 1)
                wait_past(act, s_out, 16 * kf if stored is None else stored)
                act.activation(res[:, 0:width, :].rearrange("p b d -> p (b d)"), ps[:, RES, 0:width * D],
                               ACT.Copy).then_inc(s_res, 1)

            def turn(a, r, g):
                static = isinstance(a, int)
                if r == 1 and (not static or g >= 3):
                    keep_result(g - 3)
                if not static or LEAD < a + LEAD + 1 < NB:
                    make_mask(a + LEAD + 1, (r + 1) % 2)
                late = static and a + LEAD >= NB
                if late:
                    exponentials(a)
                if not static or a >= 1:
                    keep_sum(a - 1, (r + 1) % 2)
                    keep_x2(a - 1)
                if not late:
                    exponentials(a)
                if not static or a + RINGS < NB:
                    slot_numbers(a + RINGS, r)
                if r == 2 and (not static or g >= 2):
                    gelu_up(g - 2)
                if r == 2 and (not static or g >= 1):
                    deviation(LN_B + g - 1)
                if not static or a + LEAD < NB:
                    keep_keys(a + LEAD, r % 2)
                if r == 0 and (not static or g >= 2):
                    keep_rows_T(LN_B + g - 2, ROWS, 1)

            for g in range(4):
                for r in range(G):
                    turn(G * g + r, r, g)
            with act.Fori(4, NG - 3) as g:
                for r in range(G):
                    turn(G * g + r, r, g)
            for a in range(NB - 3 * G, NB - G):
                turn(a, a % G, a // G)
            act.wait_ge(s_vadj, 16)
            act.activation(mask[:, 0, :], adj_sb[:, 0, :], ACT.Square).then_inc(s_mask, 1)
            keep_sum(NB - 5, 1)
            exponentials(NB - 4)
            keep_x2(NB - 5)
            keep_result(NG - 4)
            keep_rows_T(LN_B + NG - 3, ROWS, 1)
            act.wait_ge(s_top, NB + 1)
            act.activation(vidx[:, :], vtop[:, :], ACT.Relu, scale=-1.0, bias=col2).then_inc(s_idx, 1)
            act.activation(vgap[:, SELF:S2], vtop[:, :], ACT.Relu, scale=-1.0, bias=n_col).then_inc(s_gap, 1)

            keep_sum(NB - 4, 0)
            exponentials(NB - 3)
            keep_x2(NB - 4)
            gelu_up(NG - 3)
            deviation(LN_B + NG - 2)

            keep_sum(NB - 3, 1)
            exponentials(NB - 2)
            keep_x2(NB - 3)
            keep_result(NG - 3)
            keep_rows_T(LN_B + NG - 2, ROWS, 1)

            keep_sum(NB - 2, 0)
            exponentials(NB - 1)
            keep_x2(NB - 2)
            gelu_up(NG - 2, chunks=(0, 1))

            keep_sum(NB - 1, 1)
            keep_x2(NB - 1)
            gelu_up(NG - 2, chunks=(2, 3))
            exponentials(NB, S2)
            deviation(LN_B + NG - 1)
            keep_result(NG - 2)
            keep_sum(NB, 0)
            keep_rows_T(LN_B + NG - 1, ROWS, 1)
            keep_x2(NB)
            deviation(LN_V)
            gelu_up(NG - 1)
            keep_result(NG - 1)
            keep_rows_T(LN_V, ROWS, 1, width=1)
            gelu_up(FF_V, 1)
            keep_result(FF_V, 1)

            with where_dense(act):
                act.wait_ge(d_load, 32)
                with act.Fori(0, NB) as c:
                    act.activation(xn[:, 0, 0, :], block_of(xs, c), ACT.Copy).then_inc(d_copied, 1)
                    act.wait_ge(d_kT_ps, c + 1)
                    act.activation(kT[:, bass.ts(c, P)], ps[:, 0, 0:P], ACT.Copy).then_inc(d_kT, 1)
                with act.Fori(0, NB) as b:
                    act.activation(xn[:, 1, 0, :], block_of(qs, b), ACT.Copy).then_inc(d_q, 1)
                    act.wait_ge(d_qT_ps, b + 1)
                    act.activation(xnT[:, 0, 0:P], ps[:, 1, 0:P], ACT.Copy).then_inc(d_qT, 1)
                    with act.Fori(0, H) as h:
                        act.wait_ge(d_neg, H * b + h + 1)
                        act.activation(s_all, s_all, ACT.Exp, scale=SCALE, bias=smax[:, 1:2],
                                       accum_out=den[:, 0:1]).then_inc(d_exp, 1)
                    act.wait_ge(d_oT_ps, b + 1)
                    act.activation(oT[:, 0, :], ps[:, 0, 0:P], ACT.Copy).then_inc(d_oT, 1)
                    act.wait_ge(d_x2_ps, b + 1)
                    act.activation(block_of(xs, b), ps[:, 2, 0:D], ACT.Copy).then_inc(d_x2, 1)
                with act.Fori(0, NG) as g:
                    deviation(LN_D + g)
                    keep_rows_T(LN_D + g, ROWS, 1)
                    gelu_up(FF_D + g)
                    act.wait_ge(s_vout, 16)
                    keep_result(FF_D + g, stored=16 * (FF_D + g) - 16)

        @block.vector
        def _(dve):
            def moment_steps(k, rows, width=G, j=0, before=1):
                w = slice(0, width)
                even, odd = stats[:, j, w, 1], stats[:, j, w, 4]

                def statistics():
                    for i in range(width):
                        last = dve.bn_stats(stats[:, j, i, :], rows(i))
                    last.then_inc(s_moments, 1)

                def sums():
                    dve.wait_ge(s_moments, 7 * k + 1)
                    dve.tensor_tensor(mean[:, j, w], even, odd, ALU.add).then_inc(s_moments, 1)
                    dve.tensor_tensor(half[:, j, w], even, odd, ALU.subtract).then_inc(s_moments, 1)
                    wait_past(dve, s_sqrt, k - before + 1)
                    dve.scalar_tensor_tensor(out=var[:, j, w], in0=stats[:, j, w, 2], scalar=EPS * D,
                                             in1=stats[:, j, w, 5], op0=ALU.add, op1=ALU.add).then_inc(s_moments, 1)

                def squares():
                    dve.wait_ge(s_moments, 7 * k + 4)
                    dve.tensor_scalar(mean[:, j, w], mean[:, j, w], -0.5, None, ALU.mult).then_inc(s_moments, 1)
                    dve.scalar_tensor_tensor(out=half[:, j, w], in0=half[:, j, w], scalar=0.25, in1=half[:, j, w],
                                             op0=ALU.mult, op1=ALU.mult).then_inc(s_moments, 1)

                def variances():
                    dve.wait_ge(s_moments, 7 * k + 6)
                    dve.scalar_tensor_tensor(out=var[:, j, w], in0=var[:, j, w], scalar=1.0 / D, in1=half[:, j, w],
                                             op0=ALU.mult, op1=ALU.add).then_inc(s_moments, 1)

                return statistics, sums, squares, variances

            def moments(k, rows, width=G, j=0, before=1):
                for each in moment_steps(k, rows, width, j, before):
                    each()

            def scale_steps(k, j=0):
                def inverse():
                    dve.wait_ge(s_sqrt, k + 1)
                    dve.reciprocal(rstd[:, j, :], rstd[:, j, :]).then_inc(s_rstd, 1)

                def shifts():
                    dve.wait_ge(s_rstd, k + 1)
                    dve.tensor_tensor(shift[:, j, :], mean[:, j, :], rstd[:, j, :], ALU.mult).then_inc(s_shift, 1)

                return inverse, shifts

            def scale_rows(k, j=0):
                for each in scale_steps(k, j):
                    each()

            def normalise(k, rows, width=G, j=0, before=1):
                dve.wait_ge(s_shift, k + 1)
                wait_past(dve, s_xnT_ps, k - before + 1)
                for i in range(width):
                    last = dve.tensor_scalar(xn[:, j, i, :], rows(i), rstd[:, j, i:i + 1], shift[:, j, i:i + 1],
                                             ALU.mult, ALU.add)
                last.then_inc(s_xn, 1)

            def search(b, i, bank):
                dve.wait_ge(s_keys, NSEG * b + i + 1)
                dve.nop(nofuse=True)
                dve.max(out=cand[:, 8 * i:8 * i + 8], in_=ps[:, bank, :]).then_inc(s_cand, 1)

            def drop_self(b, j):
                dve.wait_ge(s_cand, NSEG * (b + 1))
                wait_past(dve, s_gap, 3 * (b - 1))
                dve.scalar_tensor_tensor(out=clean[:, j, :], in0=cand[:, :], scalar=self_key[:, bass.ds(b, 1)],
                                         in1=cand[:, :], op0=ALU.not_equal, op1=ALU.mult).then_inc(s_clean, 1)

            def best(b, j):
                dve.wait_ge(s_clean, b + 1)
                dve.nop(nofuse=True)
                dve.max(out=top[:, j, :], in_=clean[:, j, :]).then_inc(s_top, 1)

            dve.memset(column_key[:, :], 0.0).then_inc(s_key_rows, 1)
            for tile in (var, mean, rstd, half, shift):
                dve.memset(tile[:, :, :], 1.0)

            def input_rows(k):
                return lambda i: xs[:, G * k + i, :]

            for k in range(NG + 3):
                e = k - 2
                find = 0 <= e < LEAD
                if 1 <= k <= NG:
                    scale_rows(k - 1, (k - 1) % 2)
                    normalise(k - 1, input_rows(k - 1), j=(k - 1) % 2, before=2)
                if k >= 3:
                    dve.wait_ge(s_kv_ps, k - 2)
                    dve.tensor_copy(slots[:, G * (k - 3):G * (k - 2), :].rearrange("p b d -> p (b d)"),
                                    ps[:, A_KV:A_KV + 2, :].rearrange("p a m -> p (a m)")).then_inc(s_kv, 1)
                norm = ()
                if k < NG:
                    dve.wait_ge(s_x[k // 2], 16)
                    norm = moment_steps(k, input_rows(k), j=k % 2, before=2)
                if e == 0:
                    dve.wait_ge(s_const, KEYS_MADE)
                for i in range(NSEG):
                    if norm:
                        norm[i]()
                    if find:
                        search(e, i, A_KEYS + i)
                if find:
                    drop_self(e, e % 2)
                if find:
                    best(e, e % 2)
            dve.wait_ge(s_diag, 16)
            dve.tensor_scalar(gap[:, :, 0], diag[:, :], 0.0, None, ALU.is_equal).then_inc(s_flag, 1)
            dve.wait_ge(s_flag, 1)
            dve.wait_ge(s_q, NG)
            dve.wait_ge(s_const, NCONST)

            def group_rows(g):
                return lambda i: block_of(xs, G * g + i)

            def score_steps(b, r, q, gaps):
                tile, n = slot_tile(b, r)

                def after(step):
                    dve.wait_ge(s_score, SCORE_STEPS * b + step)

                def products():
                    dve.tensor_tensor(prod[:, 0:n, :], tile[:, :, 0:D], q.to_broadcast([P, n, D]),
                                      ALU.mult).then_inc(s_score, 1)

                def head_sums():
                    after(1)
                    wait_past(dve, s_exp, b)
                    dve.tensor_reduce(sc[:, 0:n, :].rearrange("p s h -> p (s h)"),
                                      prod[:, 0:n, :].rearrange("p s (h e) -> p (s h) e", e=DH),
                                      axis=AX_X, op=ALU.add).then_inc(s_score, 1)

                def shut_empty():
                    after(2)
                    dve.scalar_tensor_tensor(out=sc[:, 0:n, :], in0=over_heads(gaps, n), scalar=NEG,
                                             in1=sc[:, 0:n, :], op0=ALU.mult, op1=ALU.add).then_inc(s_score, 1)

                def maximum():
                    after(3)
                    dve.tensor_reduce(smax[:, :], sc[:, 0:n, :].rearrange("p s h -> p h s"), axis=AX_X,
                                      op=ALU.max).then_inc(s_score, 1)

                def less_maximum():
                    after(4)
                    dve.tensor_tensor(sc[:, 0:n, :], sc[:, 0:n, :], over_slots(smax[:, :], n),
                                      ALU.subtract).then_inc(s_score, 1)

                return products, head_sums, shut_empty, maximum, less_maximum

            def arrived(b, r):
                dve.wait_ge(s_gather[r], ring_count(b, r, 128))
                dve.wait_ge(s_self[r], ring_count(b, r, 16))
                dve.wait_ge(s_gap, 3 * (b + 1))

            def block_steps(b, r):
                return score_steps(b, r, qs[:, bass.ds(b, 1), :], block_of(gap, b))

            def denominators(b, n):
                dve.wait_ge(s_exp, b + 1)
                dve.tensor_reduce(den[:, :], ex[:, 0:n, :].rearrange("p s h -> p h s"), axis=AX_X,
                                  op=ALU.add).then_inc(s_soft, 1)

            def value_steps(b, r, n):
                tile = slot_tile(b, r)[0]

                def inverses():
                    dve.wait_ge(s_soft, 3 * b + 1)
                    dve.reciprocal(rden[:, :], den[:, :]).then_inc(s_soft, 1)

                def probabilities():
                    dve.wait_ge(s_soft, 3 * b + 2)
                    dve.tensor_tensor(pr[:, 0:n, :], ex[:, 0:n, :], over_slots(rden[:, :], n),
                                      ALU.mult).then_inc(s_soft, 1)

                def weigh():
                    dve.wait_ge(s_soft, 3 * b + 3)
                    wait_past(dve, s_oT_ps, b - 1)
                    dve.tensor_tensor(pv[r % 2][:, 0:n, :].rearrange("p s (h e) -> p s h e", e=DH),
                                      tile[:, :, D:2 * D].rearrange("p s (h e) -> p s h e", e=DH),
                                      pr[:, 0:n, :].rearrange("p s (h a) -> p s h a", a=1).to_broadcast([P, n, H, DH]),
                                      ALU.mult).then_inc(s_pv, 1)

                return inverses, probabilities, weigh

            def turn(a, r, g):
                static = isinstance(a, int)
                find = not static or a + LEAD < NB
                scores = block_steps(a, r)
                for i in range(1, SCORE_STEPS):
                    scores[i]()
                    if find:
                        search(a + LEAD, i - 1, KEY_BANKS[i - 1])
                if not static or a + 1 < NB:
                    arrived(a + 1, (r + 1) % RINGS)
                    block_steps(a + 1, (r + 1) % RINGS)[0]()
                if find:
                    drop_self(a + LEAD, r % 2)
                denominators(a, S1)
                if find:
                    best(a + LEAD, r % 2)
                norm = ()
                scale_turn = 2 if static and g == NG - 1 else 3
                if not static or g >= 1:
                    k = LN_B + g - 1
                    if r == 1:
                        dve.wait_ge(s_x2, G * g)
                        norm = moment_steps(k, group_rows(g - 1))
                    if r == scale_turn:
                        norm = scale_steps(k)
                values = value_steps(a, r, S1)
                for i in range(max(len(values), len(norm))):
                    if i < len(values):
                        values[i]()
                    if i < len(norm):
                        norm[i]()
                if r == scale_turn and (not static or g >= 1):
                    normalise(k, group_rows(g - 1))

            arrived(0, 0)
            block_steps(0, 0)[0]()
            for g in range(3):
                for r in range(G):
                    turn(G * g + r, r, g)
            with dve.Fori(3, NG - 2) as g:
                for r in range(G):
                    turn(G * g + r, r, g)
            turn(NB - LEAD, 0, NG - 2)

            flagged = [1]

            def link(instruction):
                flagged[0] += 1
                instruction.then_inc(s_flag, 1)
                dve.wait_ge(s_flag, flagged[0])

            dve.wait_ge(s_gap, 3 * NB)
            link(dve.tensor_scalar(work[:, :, :], found[:, :, :], float(HALF), None, ALU.is_ge))
            link(dve.tensor_reduce(full[:, :, :], work[:, :, :].rearrange("p b (s k) -> p b s k", k=8), axis=AX_X,
                                   op=ALU.add))
            link(dve.tensor_reduce(count[:, :], full[:, :, :], axis=AX_X, op=ALU.add))
            link(dve.tensor_scalar(flag[:, :], count[:, :], 8.5, None, ALU.is_gt))
            link(dve.tensor_reduce(worst[:, :], full[:, :, :], axis=AX_X, op=ALU.max))
            link(dve.scalar_tensor_tensor(out=flag[:, :], in0=worst[:, :], scalar=6.5, in1=flag[:, :],
                                          op0=ALU.is_ge, op1=ALU.max))
            link(dve.tensor_reduce(worst[:, :], found[:, :, :], axis=AX_X, op=ALU.max))
            link(dve.scalar_tensor_tensor(out=flag[:, :], in0=worst[:, :], scalar=float(3 * HALF), in1=flag[:, :],
                                          op0=ALU.is_ge, op1=ALU.max))
            turn(NB - LEAD + 1, 1, NG - 2)

            dve.wait_ge(s_flag_ps, 1)
            link(dve.tensor_copy(totals[:, :], ps[:, SUMS, NB:2 * NB]))
            link(dve.tensor_tensor_scan(worst[:, :], totals[:, :], totals[:, :], 0.0, ALU.add, ALU.bypass))
            link(dve.tensor_tensor(place[:, :], worst[:, :], totals[:, :], ALU.subtract))
            link(dve.tensor_tensor(place[:, :], place[:, :], ps[:, SUMS, 0:NB], ALU.add))
            link(dve.scalar_tensor_tensor(out=place[:, :], in0=place[:, :], scalar=1.0, in1=flag[:, :],
                                          op0=ALU.add, op1=ALU.mult))
            assert flagged[0] == FLAG_STEPS, flagged[0]
            for c in range(PICKS):
                w = NB // PICKS
                places = place[:, w * c:w * (c + 1)].rearrange("p (b a) -> p b a", a=1).to_broadcast([P, w, P])
                dve.tensor_tensor(pick[:, w * c:w * (c + 1), :],
                                  rank[:, :].rearrange("p (a n) -> p a n", a=1).to_broadcast([P, w, P]),
                                  places, ALU.is_equal).then_inc(s_pick, 1)
            dve.wait_ge(s_pick_ps, 1)
            vn = [0]

            def vlink(instruction):
                vn[0] += 1
                instruction.then_inc(s_vnum, 1)
                dve.wait_ge(s_vnum, vn[0])

            vlink(dve.tensor_reduce(vnum[:, 0:1], ps[:, LIST, 0:2], axis=AX_X, op=ALU.add))
            vlink(dve.tensor_scalar(vnum[:, 1:2], vnum[:, 0:1], 0.0, float(NO_ROW), ALU.is_equal, ALU.mult))
            vlink(dve.tensor_scalar(vnum[:, 2:3], vnum[:, 0:1], -1.0, COL2 + 1.0, ALU.mult, ALU.add))
            dve.scalar_tensor_tensor(out=vrow[:, :], in0=vnum[:, 0:1], scalar=-1.0, in1=vnum[:, 1:2],
                                     op0=ALU.add, op1=ALU.add).then_inc(s_vrow, 1)
            for a in range(NB - 6, NB - 3):
                turn(a, a % G, a // G)

            for s in range(VSEG):
                dve.wait_ge(s_keys, ALL_KEYS + s + 1)
                dve.max(out=vcand[:, 8 * s:8 * s + 8], in_=ps[:, KEYS + s % RING, :]).then_inc(s_cand, 1)
            dve.wait_ge(s_cand, ALL_KEYS + VSEG)
            vs = [0]

            def slink(instruction):
                vs[0] += 1
                instruction.then_inc(s_vsearch, 1)
                dve.wait_ge(s_vsearch, vs[0])

            slink(dve.scalar_tensor_tensor(out=vclean[:, :], in0=vcand[:, :], scalar=vnum[:, 2:3], in1=vcand[:, :],
                                           op0=ALU.not_equal, op1=ALU.mult))
            slink(dve.max(out=vtop[:, 0:8], in_=vclean[:, :]))
            slink(dve.match_replace(out=vrest[:, :], in_to_replace=vtop[:, 0:8], in_values=vclean[:, :],
                                    imm_value=-1.0))
            dve.max(out=vtop[:, 8:16], in_=vrest[:, :]).then_inc(s_top, 1)
            slink(dve.tensor_scalar(vwork[:, :], vcand[:, :], vnum[:, 2:3], None, ALU.is_equal))
            slink(dve.tensor_reduce(vstat[:, 0:1], vwork[:, :], axis=AX_X, op=ALU.add))
            slink(dve.tensor_scalar(vgap[:, 0:1], vstat[:, 0:1], -1.0, 1.0, ALU.mult, ALU.add))
            slink(dve.tensor_scalar(vwork[:, :], vclean[:, :], float(N), None, ALU.is_ge))
            slink(dve.tensor_reduce(vstat[:, 1:2], vwork[:, :], axis=AX_X, op=ALU.add))
            slink(dve.tensor_reduce(vstat[:, 2:3], vcand[:, 7::8], axis=AX_X, op=ALU.max))
            slink(dve.tensor_reduce(vstat[:, 3:4], vcand[:, :], axis=AX_X, op=ALU.max))
            slink(dve.tensor_scalar(vstat[:, 4:5], vstat[:, 1:2], 16.5, None, ALU.is_gt))
            slink(dve.scalar_tensor_tensor(out=vstat[:, 4:5], in0=vstat[:, 2:3], scalar=float(N), in1=vstat[:, 4:5],
                                           op0=ALU.is_ge, op1=ALU.max))
            slink(dve.scalar_tensor_tensor(out=vstat[:, 4:5], in0=vstat[:, 3:4], scalar=float(2 * N),
                                           in1=vstat[:, 4:5], op0=ALU.is_ge, op1=ALU.max))
            slink(dve.scalar_tensor_tensor(out=vstat[:, 4:5], in0=vnum[:, 0:1], scalar=0.0, in1=vstat[:, 4:5],
                                           op0=ALU.is_gt, op1=ALU.mult))
            dve.scalar_tensor_tensor(out=vstat[:, 5:6], in0=worst[:, NB - 1:NB], scalar=P + 0.5, in1=vstat[:, 4:5],
                                     op0=ALU.is_gt, op1=ALU.max).then_inc(s_vcheck, 1)
            for a in range(NB - 3, NB):
                turn(a, a % G, a // G)

            dve.wait_ge(s_vcheck_ps, 1)
            dve.tensor_scalar(dense_flag[:, :], ps[:, CHECK, 0:1], -1.0 if force_dense else 0.5, None,
                              ALU.is_gt).then_inc(s_dense, 1)
            k = LN_B + NG - 1
            dve.wait_ge(s_vload, 48)
            dve.wait_ge(s_vgather, 256)
            dve.wait_ge(s_gap, 3 * NB + 1)
            scores = score_steps(NB, 0, vq[:, :, :], vgap[:, :])
            for each in scores:
                each()
            dve.wait_ge(s_x2, NB)
            moments(k, group_rows(NG - 1))
            denominators(NB, S2)
            for each in value_steps(NB, 0, S2):
                each()
            scale_rows(k)
            normalise(k, group_rows(NG - 1))
            dve.wait_ge(s_x2, NB + 1)
            moments(LN_V, group_rows(NG), 1)
            scale_rows(LN_V)
            normalise(LN_V, group_rows(NG), 1)

            with where_dense(dve):
                dve.memset(smax[:, 0:1], 0.0).then_inc(d_adj_free, 1)
                with dve.Fori(0, NB) as b:
                    dve.wait_ge(d_adj, 16 * b + 16)
                    dve.tensor_scalar(bias, adj_sb[:, 0, :], 0.0, NEG, ALU.is_equal, ALU.mult).then_inc(d_bias, 1)
                    dve.wait_ge(d_bias, b + 1)
                    dve.memset(smax[:, 0:1], 0.0).then_inc(d_adj_free, 1)
                    dve.wait_ge(d_qT, b + 1)
                    dve.nop(nofuse=True)
                    with dve.Fori(0, H) as h:
                        t = H * b + h + 1
                        dve.tensor_scalar(xnT[:, 1, 0:P], xnT[:, 0, 0:P], head_cols[:, bass.ds(h, 1)], None,
                                          ALU.mult).then_inc(d_qh, 1)
                        dve.wait_ge(d_s_ps, t)
                        dve.tensor_tensor(s_all, ps[:, :, :].rearrange("p a m -> p (a m)"), bias,
                                          ALU.add).then_inc(d_s, 1)
                        dve.wait_ge(d_s, t)
                        dve.tensor_reduce(smax[:, 0:1], s_all, axis=AX_X, op=ALU.max).then_inc(d_max, 1)
                        dve.wait_ge(d_max, t)
                        dve.tensor_scalar(smax[:, 1:2], smax[:, 0:1], -SCALE, None, ALU.mult).then_inc(d_neg, 1)
                        dve.wait_ge(d_exp, t)
                        dve.reciprocal(rden[:, 0:1], den[:, 0:1]).then_inc(d_rden, 1)
                        for c in range(TURNS):
                            dve.wait_ge(d_pT_ps, TURNS * (t - 1) + c + 1)
                            dve.tensor_copy(pT[:, c % 2, :], ps[:, c % 2, :]).then_inc(d_pT, 1)
                        dve.wait_ge(d_o_ps, t)
                        dve.wait_ge(d_rden, t)
                        dve.tensor_scalar(att[:, bass.ts(h, DH)], ps[:, 7, 0:DH], rden[:, 0:1], None,
                                          ALU.mult).then_inc(d_o, 1)
                dve.wait_ge(d_x2, NB)
                with dve.Fori(0, NG) as g:
                    moments(LN_D + g, group_rows(g))
                    scale_rows(LN_D + g)
                    normalise(LN_D + g, group_rows(g))

        @block.tensor
        def _(pe):
            def transpose_rows(k, bank, j=0, width=G):
                pe.wait_ge(s_xn, k + 1)
                for i in range(width):
                    last = pe.transpose(ps[:, bank, i * P:(i + 1) * P], xn[:, j, i, :], ident[:, :])
                last.then_inc(s_xnT_ps, 1)

            def project(c):
                j = c % 2
                pe.wait_ge(s_xnT, c + 1)
                wait_past(pe, s_q, c)
                for i in range(G):
                    last = pe.matmul(ps[:, A_Q, i * D:(i + 1) * D], xnT[:, j, i * P:(i + 1) * P],
                                     wqkv_sb[:, 0:D], start=True, stop=True)
                last.then_inc(s_q_ps, 1)
                wait_past(pe, s_kv, c)
                for i in range(G):
                    last = pe.matmul(ps[:, A_KV + i // 2, 2 * D * (i % 2):2 * D * (i % 2 + 1)],
                                     xnT[:, j, i * P:(i + 1) * P], wqkv_sb[:, D:3 * D], start=True, stop=True)
                last.then_inc(s_kv_ps, 1)

            def key_segment(b, i, j, bank):
                low, high = slice(SEG * i, SEG * (i + 1)), slice(HALF + SEG * i, HALF + SEG * (i + 1))
                out = ps[:, bank, :]
                pe.matmul(out, ident_2[:, :], mask[:, j, low], start=True, stop=False)
                pe.matmul(out, ident_1[:, :], mask[:, j, high], start=False, stop=False)
                pe.matmul(out, ones33[:, :], column_key[:, high], start=False, stop=True).then_inc(s_keys, 1)

            def keys(b, j, banks, ring, segments=range(NSEG)):
                pe.wait_ge(s_mask, b + 1)
                for i in segments:
                    before_it = i - ring if i >= ring else (NSEG - 1) // ring * ring + i
                    if before_it >= NSEG:
                        before_it -= ring
                    wait_past(pe, s_cand, NSEG * (b if i >= ring else b - 1) + before_it + 1)
                    key_segment(b, i, j, banks[i])

            pe.wait_ge(s_const, IDENT_MADE)
            pe.wait_ge(s_wqkv, 16 * NWQKV)
            for k in range(1, NG + 3):
                e = k - 2
                if 1 <= e < LEAD:
                    keys(e, e % 2, [A_KEYS + i for i in range(NSEG)], NSEG)
                if k <= NG:
                    wait_past(pe, s_xnT, k - 1)
                    transpose_rows(k - 1, A_ROWS, (k - 1) % 2)
                if 0 <= k - 2 < NG:
                    project(k - 2)
                if e == 0:
                    pe.wait_ge(s_const, KEYS_MADE)
                    keys(0, 0, [A_KEYS + i for i in range(NSEG)], NSEG)
            pe.wait_ge(s_q, NG)
            pe.wait_ge(s_kv, NG)
            pe.wait_ge(s_cand, NSEG * LEAD)
            pe.wait_ge(s_const, NCONST)
            pe.wait_ge(s_weights, 16 * NWEIGHTS)

            def sum_slots(b, j, n=S1):
                wait_past(pe, s_x2, b)
                pe.wait_ge(s_pv, b + 1)
                for s in range(n):
                    last = pe.matmul(ps[:, ATT, 0:P], pv[j][:, s, :], ident[:, :], start=(s == 0), stop=(s == n - 1))
                last.then_inc(s_oT_ps, 1)

            def attention_out(b, j):
                pe.wait_ge(s_oT, b + 1)
                pe.matmul(ps[:, ATT, P:P + D], ident[:, :], block_of(xs, b), start=True, stop=False)
                pe.matmul(ps[:, ATT, P:P + D], ones[0:1, :], bproj_row[:, :], start=False, stop=False)
                pe.matmul(ps[:, ATT, P:P + D], oT[:, j, :], wproj_sb[:, :], start=False, stop=True).then_inc(s_x2_ps, 1)

            def up(kf, k, chunks=range(FC), width=G):
                pe.wait_ge(s_xnT, k + 1)
                for c in chunks:
                    if c == 1:
                        wait_past(pe, s_res, kf)
                    else:
                        wait_past(pe, s_g, FC * kf)
                    pe.matmul(ps[:, UP_BANKS[c], 0:width * P], w1_sb[:, c * P:(c + 1) * P],
                              xnT[:, 0, 0:width * P], start=True, stop=True).then_inc(s_u_ps, 1)

            def down(kf, g, blocks, last_blocks):
                pe.wait_ge(s_g, FC * kf + FC)
                for i in blocks:
                    bank = ps[:, RES, i * D:(i + 1) * D]
                    for c in range(FC):
                        pe.matmul(bank, gT[:, c, i * P:(i + 1) * P], w2_sb[:, c, :], start=(c == 0), stop=False)
                    pe.matmul(bank, ones[0:1, :], b2_row[:, :], start=False, stop=False)
                    last = pe.matmul(bank, ident[:, :], block_of(xs, G * g + i), start=False, stop=True)
                if last_blocks:
                    last.then_inc(s_ff, 1)

            def turn(a, r, g):
                static = isinstance(a, int)
                if not static or a + LEAD < NB:
                    keys(a + LEAD, r % 2, KEY_BANKS, RING, range(RING))
                if not static or a >= 1:
                    sum_slots(a - 1, (r + 1) % 2)
                if not static or a + LEAD < NB:
                    keys(a + LEAD, r % 2, KEY_BANKS, RING, range(RING, NSEG))
                late = static and a + LEAD >= NB
                if not late and (not static or a >= 1):
                    attention_out(a - 1, (r + 1) % 2)
                if r == 0 and (not static or g >= 3):
                    down(g - 3, g - 3, range(2, G), True)
                if r == 0 and (not static or g >= 2):
                    transpose_rows(LN_B + g - 2, ROWS)
                if r in (1, 2) and (not static or g >= 2):
                    up(g - 2, LN_B + g - 2, ((0, 1), (2, 3))[r - 1])
                if r == 3 and (not static or g >= 2):
                    down(g - 2, g - 2, range(2), False)
                if late:
                    attention_out(a - 1, (r + 1) % 2)

            for g in range(4):
                for r in range(G):
                    turn(G * g + r, r, g)
            with pe.Fori(4, NG - 2) as g:
                for r in range(G):
                    turn(G * g + r, r, g)
            turn(NB - LEAD, 0, NG - 2)
            pe.wait_ge(s_flag, 9)
            pe.wait_ge(s_cand, ALL_KEYS)
            pe.matmul(ps[:, SUMS, 0:NB], before[:, :], flag[:, :], start=True, stop=True)
            pe.matmul(ps[:, SUMS, NB:2 * NB], ones[:, :], flag[:, :], start=True, stop=True).then_inc(s_flag_ps, 1)
            turn(NB - LEAD + 1, 1, NG - 2)
            for b in range(NB):
                if b % (NB // PICKS) == 0:
                    pe.wait_ge(s_pick, b // (NB // PICKS) + 1)
                last = pe.matmul(ps[:, LIST, 0:2], pick[:, b, :], row_number[:, b, :], start=(b == 0),
                                 stop=(b == NB - 1))
            last.then_inc(s_pick_ps, 1)
            for a in range(NB - 6, NB - 4):
                turn(a, a % G, a // G)
            sum_slots(NB - 5, 1)
            attention_out(NB - 5, 1)
            down(NG - 4, NG - 4, range(2, G), True)
            transpose_rows(LN_B + NG - 3, ROWS)
            pe.wait_ge(s_vnum, 1)
            pe.wait_ge(s_mask, NB + 1)
            for s in range(VSEG):
                pe.wait_ge(s_cand, ALL_KEYS + s - RING + 1)
                cols = slice(SEG * s, SEG * (s + 1))
                pe.matmul(ps[:, KEYS + s % RING, :], ident_2[:, :], mask[:, 0, cols], start=True, stop=False)
                pe.matmul(ps[:, KEYS + s % RING, :], ones33[:, :], column_key[:, cols], start=False,
                          stop=True).then_inc(s_keys, 1)

            sum_slots(NB - 4, 0)
            attention_out(NB - 4, 0)
            up(NG - 3, LN_B + NG - 3)
            pe.wait_ge(s_vcheck, 1)
            pe.wait_ge(s_cand, ALL_KEYS + VSEG)
            pe.matmul(ps[:, CHECK, 0:1], ones[:, :], vstat[:, 5:6], start=True, stop=True).then_inc(s_vcheck_ps, 1)

            sum_slots(NB - 3, 1)
            attention_out(NB - 3, 1)
            down(NG - 3, NG - 3, range(G), True)
            transpose_rows(LN_B + NG - 2, ROWS)

            sum_slots(NB - 2, 0)
            attention_out(NB - 2, 0)
            up(NG - 2, LN_B + NG - 2, (0, 1))

            sum_slots(NB - 1, 1)
            attention_out(NB - 1, 1)
            up(NG - 2, LN_B + NG - 2, (2, 3))
            down(NG - 2, NG - 2, range(G), True)
            sum_slots(NB, 0, S2)
            transpose_rows(LN_B + NG - 1, ROWS)
            attention_out(NB, 0)
            up(NG - 1, LN_B + NG - 1)
            down(NG - 1, NG - 1, range(G), True)
            transpose_rows(LN_V, ROWS, width=1)
            up(FF_V, LN_V, width=1)
            down(FF_V, NG, range(1), True)

            with where_dense(pe):
                with pe.Fori(0, NB) as c:
                    pe.wait_ge(d_copied, c + 1)
                    pe.transpose(ps[:, 0, 0:P], xn[:, 0, 0, :], ident[:, :]).then_inc(d_kT_ps, 1)
                pe.wait_ge(d_kT, NB)
                pe.wait_ge(d_x, 16)
                with pe.Fori(0, NB) as b:
                    pe.wait_ge(d_q, b + 1)
                    pe.transpose(ps[:, 1, 0:P], xn[:, 1, 0, :], ident[:, :]).then_inc(d_qT_ps, 1)
                    with pe.Fori(0, H) as h:
                        t = H * b + h + 1
                        pe.wait_ge(d_qh, t)
                        for c in range(TURNS):
                            last = pe.matmul(ps[:, c, :], xnT[:, 1, 0:P], kT[:, bass.ts(c, 512)], start=True, stop=True)
                        last.then_inc(d_s_ps, 1)
                        pe.wait_ge(d_exp, t)
                        for c in range(TURNS + 1):
                            if c < TURNS:
                                if c >= 2:
                                    pe.wait_ge(d_pT, TURNS * (t - 1) + c - 1)
                                for r in range(4):
                                    last = pe.transpose(ps[:, c % 2, bass.ts(r, P)],
                                                        s_all[:, bass.ts(4 * c + r, P)], ident[:, :])
                                last.then_inc(d_pT_ps, 1)
                            if c >= 1:
                                pe.wait_ge(d_pT, TURNS * (t - 1) + c)
                                for r in range(4):
                                    m = 4 * (c - 1) + r
                                    last = pe.matmul(ps[:, 7, 0:DH], pT[:, (c - 1) % 2, bass.ts(r, P)],
                                                     v_all[:, m, bass.ts(h, DH)], start=(m == 0), stop=(m == NB - 1))
                        last.then_inc(d_o_ps, 1)
                    pe.wait_ge(d_o, H * b + H)
                    pe.transpose(ps[:, 0, 0:P], att, ident[:, :]).then_inc(d_oT_ps, 1)
                    pe.matmul(ps[:, 2, 0:D], ident[:, :], block_of(xs, b), start=True, stop=False)
                    pe.matmul(ps[:, 2, 0:D], ones[0:1, :], bproj_row[:, :], start=False, stop=False)
                    pe.wait_ge(d_oT, b + 1)
                    pe.matmul(ps[:, 2, 0:D], oT[:, 0, :], wproj_sb[:, :], start=False, stop=True).then_inc(d_x2_ps, 1)
                pe.wait_ge(d_x2, NB)
                with pe.Fori(0, NG) as g:
                    transpose_rows(LN_D + g, ROWS)
                    up(FF_D + g, LN_D + g)
                    down(FF_D + g, g, range(G), True)


_INS = ["x", "adj", "L0_gnn_w_qkv", "L0_gnn_w_proj", "L0_gnn_b_proj", "L0_gnn_w1", "L0_gnn_b1", "L0_gnn_w2",
        "L0_gnn_b2", "L0_gnn_g1", "L0_gnn_be1", "L0_gnn_g2", "L0_gnn_be2"]


def kernel(**inputs):
    import numpy as _np
    import concourse.bacc as _bacc
    from concourse import mybir as _mybir
    from concourse.bass_utils import run_bass_kernel_spmd as _run

    nc = _bacc.Bacc("TRN2", target_bir_lowering=False, num_devices=1)
    arrays, args = {}, []
    for name in _INS:
        a = _np.ascontiguousarray(inputs[name])
        arrays[f"in_{name}"] = a
        args.append(nc.dram_tensor(f"in_{name}", a.shape, _mybir.dt.from_np(a.dtype), kind="ExternalInput").ap())
    out = nc.dram_tensor("out_rows", (N, D), F32, kind="ExternalOutput").ap()
    graph_layer(nc, *args, out)
    r = _run(nc, [arrays], core_ids=[0])
    return r.results[0]["out_rows"]
```
